# Optimizing a Trainium2 kernel written in Bass

```python
import numpy as np
import jax
import jax.numpy as jnp

def _softmax(x, axis=-1):
    return jax.nn.softmax(x, axis=axis)

def _gelu(x):
    return jax.nn.gelu(x, approximate=True)

def _silu(x):
    return jax.nn.silu(x)

def _sigmoid(x):
    return jax.nn.sigmoid(x)

def _layernorm(x, axis=-1, eps=1e-05):
    m = jnp.mean(x, axis=axis, keepdims=True)
    v = jnp.var(x, axis=axis, keepdims=True)
    return (x - m) / jnp.sqrt(v + eps)

def _scatter_add(tgt, idx, src, axis=0):
    return tgt.at[idx].add(src)

def _segment_sum(src, seg, n):
    return jax.ops.segment_sum(src, seg, n)
kernel_name = 'mk_seq_postln_d1_jaxref_r8_00c926'

def setup_inputs(seed: int=0):
    np.random.seed(seed)
    _w = jnp.asarray

    def _L0_attn_setup():
        import jax, jax.numpy as jnp
        import numpy as np
        H = 16
        W = 32
        D_MODEL = 128
        D_FF = 512
        EPS = 1e-05

        def _layernorm(x, g, b):
            mu = jnp.mean(x, axis=-1, keepdims=True)
            var = jnp.mean(jnp.square(x - mu), axis=-1, keepdims=True)
            return (x - mu) * jax.lax.rsqrt(var + EPS) * g + b

        def _sliding_attn(q, k, v, w):
            B, Hh, S, d = q.shape
            nc = S // w
            qc = q.reshape(B, Hh, nc, w, d)
            kp = jnp.pad(k, ((0, 0), (0, 0), (w, w), (0, 0)))
            vp = jnp.pad(v, ((0, 0), (0, 0), (w, w), (0, 0)))
            idx = (jnp.arange(nc) * w)[:, None] + jnp.arange(3 * w)[None, :]
            kc = kp[:, :, idx, :]
            vc = vp[:, :, idx, :]
            scores = jnp.einsum('bhcqd,bhckd->bhcqk', qc, kc)
            q_pos = jnp.arange(nc)[:, None, None] * w + jnp.arange(w)[None, :, None]
            k_pos = jnp.arange(nc)[:, None, None] * w - w + jnp.arange(3 * w)[None, None, :]
            rel = k_pos - q_pos
            valid = (jnp.abs(rel) <= w) & (k_pos >= 0) & (k_pos < S)
            scores = jnp.where(valid[None, None], scores, jnp.float32(-1000000000.0))
            p = jax.nn.softmax(scores, axis=-1)
            out = jnp.einsum('bhcqk,bhckd->bhcqd', p, vc)
            return out.reshape(B, Hh, S, d)
        key = jax.random.key(seed)
        ks = jax.random.split(key, 8)
        B, S = (2, 512)
        src = jax.random.normal(ks[0], (B, S, D_MODEL), dtype=jnp.float32)
        ln1_g = jnp.ones((D_MODEL,), jnp.float32)
        ln1_b = jnp.zeros((D_MODEL,), jnp.float32)
        ln2_g = jnp.ones((D_MODEL,), jnp.float32)
        ln2_b = jnp.zeros((D_MODEL,), jnp.float32)
        W1 = jax.random.normal(ks[1], (D_MODEL, D_FF), jnp.float32) * 0.02
        b1 = jnp.zeros((D_FF,), jnp.float32)
        W2 = jax.random.normal(ks[2], (D_FF, D_MODEL), jnp.float32) * 0.02
        b2 = jnp.zeros((D_MODEL,), jnp.float32)
        return {'src': src, 'ln1_g': ln1_g, 'ln1_b': ln1_b, 'ln2_g': ln2_g, 'ln2_b': ln2_b, 'W1': W1, 'b1': b1, 'W2': W2, 'b2': b2}
    _L0_attn_in = _L0_attn_setup()

    def _L0_ffn_setup():
        import jax, jax.numpy as jnp
        import numpy as np
        H = 8
        KD = 128
        TOPK = 8
        NUM_KEYS = 32
        N_EXPERTS = NUM_KEYS * NUM_KEYS
        N_DIM = 128
        BN_EPS = 1e-05

        def gelu_new(x):
            c = jnp.sqrt(jnp.asarray(2.0 / jnp.pi, x.dtype))
            return 0.5 * x * (1.0 + jnp.tanh(c * (x + 0.044715 * x * x * x)))
        key = jax.random.key(seed)
        ks = jax.random.split(key, 5)
        b, s = (2, 128)
        x = jax.random.normal(ks[0], (b, s, N_DIM), dtype=jnp.float32)
        w_q = jax.random.normal(ks[1], (N_DIM, 2 * H * KD), dtype=jnp.float32) * 0.02
        bn_gamma = jnp.ones((2 * H * KD,), dtype=jnp.float32)
        bn_beta = jnp.zeros((2 * H * KD,), dtype=jnp.float32)
        keys = jax.random.normal(ks[2], (H, NUM_KEYS, 2, KD), dtype=jnp.float32) * 0.02
        down_embed = jax.random.normal(ks[3], (N_EXPERTS, N_DIM), dtype=jnp.float32) * 0.02
        up_embed = jax.random.normal(ks[4], (N_EXPERTS, N_DIM), dtype=jnp.float32) * 0.02
        return {'x': x, 'w_q': w_q, 'bn_gamma': bn_gamma, 'bn_beta': bn_beta, 'keys': keys, 'down_embed': down_embed, 'up_embed': up_embed}
    _L0_ffn_in = _L0_ffn_setup()
    _d = {'L0_attn_src': _L0_attn_in['src'], 'L0_attn_ln1_g': _L0_attn_in['ln1_g'], 'L0_attn_ln1_b': _L0_attn_in['ln1_b'], 'L0_attn_ln2_g': _L0_attn_in['ln2_g'], 'L0_attn_ln2_b': _L0_attn_in['ln2_b'], 'L0_attn_W1': _L0_attn_in['W1'], 'L0_attn_b1': _L0_attn_in['b1'], 'L0_attn_W2': _L0_attn_in['W2'], 'L0_attn_b2': _L0_attn_in['b2'], 'L0_ffn_w_q': _L0_ffn_in['w_q'], 'L0_ffn_bn_gamma': _L0_ffn_in['bn_gamma'], 'L0_ffn_bn_beta': _L0_ffn_in['bn_beta'], 'L0_ffn_keys': _L0_ffn_in['keys'], 'L0_ffn_down_embed': _L0_ffn_in['down_embed'], 'L0_ffn_up_embed': _L0_ffn_in['up_embed']}
    _x0 = _d['L0_attn_src']
    _d['L0_attn_src'] = jax.random.normal(jax.random.fold_in(jax.random.key(seed), 1), (4, 1024, 128), dtype=_x0.dtype)
    del _x0
    return _d

def reference(L0_attn_src, L0_attn_ln1_g, L0_attn_ln1_b, L0_attn_ln2_g, L0_attn_ln2_b, L0_attn_W1, L0_attn_b1, L0_attn_W2, L0_attn_b2, L0_ffn_w_q, L0_ffn_bn_gamma, L0_ffn_bn_beta, L0_ffn_keys, L0_ffn_down_embed, L0_ffn_up_embed):

    def _L0_attn_ref(src, ln1_g, ln1_b, ln2_g, ln2_b, W1, b1, W2, b2):
        import jax, jax.numpy as jnp
        import numpy as np
        H = 16
        W = 32
        D_MODEL = 128
        D_FF = 512
        EPS = 1e-05

        def _layernorm(x, g, b):
            mu = jnp.mean(x, axis=-1, keepdims=True)
            var = jnp.mean(jnp.square(x - mu), axis=-1, keepdims=True)
            return (x - mu) * jax.lax.rsqrt(var + EPS) * g + b

        def _sliding_attn(q, k, v, w):
            B, Hh, S, d = q.shape
            nc = S // w
            qc = q.reshape(B, Hh, nc, w, d)
            kp = jnp.pad(k, ((0, 0), (0, 0), (w, w), (0, 0)))
            vp = jnp.pad(v, ((0, 0), (0, 0), (w, w), (0, 0)))
            idx = (jnp.arange(nc) * w)[:, None] + jnp.arange(3 * w)[None, :]
            kc = kp[:, :, idx, :]
            vc = vp[:, :, idx, :]
            scores = jnp.einsum('bhcqd,bhckd->bhcqk', qc, kc)
            q_pos = jnp.arange(nc)[:, None, None] * w + jnp.arange(w)[None, :, None]
            k_pos = jnp.arange(nc)[:, None, None] * w - w + jnp.arange(3 * w)[None, None, :]
            rel = k_pos - q_pos
            valid = (jnp.abs(rel) <= w) & (k_pos >= 0) & (k_pos < S)
            scores = jnp.where(valid[None, None], scores, jnp.float32(-1000000000.0))
            p = jax.nn.softmax(scores, axis=-1)
            out = jnp.einsum('bhcqk,bhckd->bhcqd', p, vc)
            return out.reshape(B, Hh, S, d)
        B, S, _ = src.shape
        d_head = D_MODEL // H
        qkv = src.reshape(B, S, H, d_head).transpose(0, 2, 1, 3)
        attn = _sliding_attn(qkv, qkv, qkv, W)
        attn = attn.transpose(0, 2, 1, 3).reshape(B, S, D_MODEL)
        x = _layernorm(src + attn, ln1_g, ln1_b)
        ff = jnp.maximum(x @ W1 + b1, 0.0) @ W2 + b2
        return _layernorm(x + ff, ln2_g, ln2_b)

    def _L0_ffn_ref(x, w_q, bn_gamma, bn_beta, keys, down_embed, up_embed):
        import jax, jax.numpy as jnp
        import numpy as np
        H = 8
        KD = 128
        TOPK = 8
        NUM_KEYS = 32
        N_EXPERTS = NUM_KEYS * NUM_KEYS
        N_DIM = 128
        BN_EPS = 1e-05

        def gelu_new(x):
            c = jnp.sqrt(jnp.asarray(2.0 / jnp.pi, x.dtype))
            return 0.5 * x * (1.0 + jnp.tanh(c * (x + 0.044715 * x * x * x)))
        b, n, d = x.shape
        q = jnp.einsum('bnd,de->bne', x, w_q)
        mean = jnp.mean(q, axis=(0, 1))
        var = jnp.var(q, axis=(0, 1))
        q = (q - mean) * jax.lax.rsqrt(var + BN_EPS) * bn_gamma + bn_beta
        q = q.reshape(b, n, 2, H, KD).transpose(2, 0, 1, 3, 4)
        sim = jnp.einsum('pbnhd,hkpd->pbnhk', q, keys)
        sx, ix = jax.lax.top_k(sim[0], TOPK)
        sy, iy = jax.lax.top_k(sim[1], TOPK)
        all_scores = (sx[..., :, None] + sy[..., None, :]).reshape(b, n, H, TOPK * TOPK)
        all_indices = (ix[..., :, None] * NUM_KEYS + iy[..., None, :]).reshape(b, n, H, TOPK * TOPK)
        scores, pk = jax.lax.top_k(all_scores, TOPK)
        indices = jnp.take_along_axis(all_indices, pk, axis=-1)
        wd = down_embed[indices]
        wu = up_embed[indices]
        h = jnp.einsum('bnd,bnhkd->bnhk', x, wd)
        h = gelu_new(h)
        h = jax.nn.softmax(scores, axis=-1) * h
        out = jnp.einsum('bnhk,bnhkd->bnd', h, wu)
        return out
    x = L0_attn_src
    x = _layernorm(x + _L0_attn_ref(x, L0_attn_ln1_g, L0_attn_ln1_b, L0_attn_ln2_g, L0_attn_ln2_b, L0_attn_W1, L0_attn_b1, L0_attn_W2, L0_attn_b2), axis=-1)
    x = _layernorm(x + _L0_ffn_ref(x, L0_ffn_w_q, L0_ffn_bn_gamma, L0_ffn_bn_beta, L0_ffn_keys, L0_ffn_down_embed, L0_ffn_up_embed), axis=-1)
    return x

_drawn_inputs = setup_inputs


def setup_inputs(seed=0):
    import zlib

    import numpy as np

    out = dict(_drawn_inputs(seed))
    spreads = {'L0_attn_ln1_g': (1.0, 0.2),
     'L0_attn_ln1_b': (0.0, 0.1),
     'L0_attn_ln2_g': (1.0, 0.2),
     'L0_attn_ln2_b': (0.0, 0.1),
     'L0_attn_b1': (0.0, 0.475),
     'L0_attn_b2': (0.0, 0.1),
     'L0_ffn_bn_gamma': (1.0, 0.6),
     'L0_ffn_bn_beta': (0.0, 0.8)}
    factors = {'L0_ffn_w_q': 8.0, 'L0_ffn_keys': 8.0, 'L0_ffn_down_embed': 8.0, 'L0_ffn_up_embed': 8.0}
    for name, (base, spread) in spreads.items():
        noise = np.random.default_rng([zlib.crc32(name.encode()), seed]).standard_normal(out[name].shape)
        drawn = base * np.exp(spread * noise) if base else spread * noise
        out[name] = jnp.asarray(drawn.astype(out[name].dtype))
    for name, factor in factors.items():
        out[name] = (out[name] * factor).astype(out[name].dtype)
    return out
```

```python
from contextlib import ExitStack

import concourse.bass as bass
from concourse import mybir

ALU = mybir.AluOpType
ACT = mybir.ActivationFunctionType
AX_X = mybir.AxisListType.X
F32 = mybir.dt.float32
BF16 = mybir.dt.bfloat16
F16 = mybir.dt.float16

P = 128
HEADS = 16
DH = 8
W = 32
WIN = 3 * W
GROUPS = 4
BLOCKS = P // W
VW = 33
FF = 512
FC = FF // P
PK_HEADS = 8
KEYS = 32
TOPK = 8
EXPERTS = KEYS * KEYS
EC = EXPERTS // P
PH = 2 * PK_HEADS
EPS = 1e-5
MASKED = -1e30
FAR = -200.0
SLACK = 2.0 ** -21


def attention_and_product_keys(nc, x, x_wrapped, ln1_g, ln1_b, ln2_g, ln2_b, w1, b1, w2, b2, w_q, w_qT,
                               gamma, beta, keysT, downT, up, out):
    tokens = x.shape[0]
    NT = tokens // P
    NQ = NT // 4
    TB = 8
    PAIRS = NT // 2

    with ExitStack() as ctx:
        def sb(name, shape, dt=F32):
            return ctx.enter_context(nc.sbuf_tensor(name, shape, dt))

        def sem(name):
            return ctx.enter_context(nc.semaphore(name))

        def two(name, shape, dt=F32):
            return [sb(f"{name}{p}", shape, dt) for p in range(2)]

        def two_sems(name):
            return [sem(f"{name}{p}") for p in range(2)]

        ps = ctx.enter_context(nc.psum_tensor("ps", [P, 8, 512], F32))

        ident = sb("ident", [P, P])
        ident_bf = sb("ident_bf", [P, P], BF16)
        ident_h = sb("ident_h", [P, P], F16)
        ones = sb("ones", [P, P])
        zeros = sb("zeros", [P, P + 1], BF16)
        minus_half = sb("minus_half", [P, 16])
        fold4 = sb("fold4", [P, W])
        spread4 = sb("spread4", [W, P])
        quadrant = sb("quadrant", [P, 4])
        head16 = sb("head16", [P, HEADS])
        head_in_group = sb("head_in_group", [P, 4])
        band = sb("band", [W, WIN])
        mask = sb("mask", [P, TB * BLOCKS * WIN], BF16)
        spread_keys = sb("spread_keys", [P, EXPERTS], F16)
        ln1_g_all = sb("ln1_g_all", [P, P])
        ln1_b_all = sb("ln1_b_all", [P, P])
        ln2_g_all = sb("ln2_g_all", [P, P])
        ln2_b_all = sb("ln2_b_all", [P, P])
        b2_all = sb("b2_all", [P, P])
        b1_col = sb("b1_col", [P, FC])
        w1_sb = sb("w1_sb", [P, FF])
        w2_sb = sb("w2_sb", [P, FC, P])
        wq_sb = sb("wq_sb", [P, PH * P])
        wqT_sb = sb("wqT_sb", [P, PH, P])
        keysT_sb = sb("keysT_sb", [P, PH, KEYS])
        gamma_sb = sb("gamma_sb", [P, PH])
        beta_sb = sb("beta_sb", [P, PH])
        downT_sb = sb("downT_sb", [P, EXPERTS])
        up_sb = sb("up_sb", [P, EC, P])

        xT = sb("xT", [P, W + tokens + W])
        kept = sb("kept", [P, tokens])

        x4 = two("x4", [P, 4, P])
        window = two("window", [P, P + 2 * W])
        queries = two("queries", [P, BLOCKS, 4, W])
        v_raw = two("v_raw", [WIN, BLOCKS, P])
        v_ones = two("v_ones", [WIN, BLOCKS, GROUPS, VW])
        x_tile = two("x_tile", [P, P])
        row_max = two("row_max", [P, GROUPS * BLOCKS])
        shifted = two("shifted", [P, GROUPS * BLOCKS, WIN])
        probs = two("probs", [P, GROUPS * BLOCKS, WIN])
        probsT = [sb(f"probsT{g}", [WIN, BLOCKS, P]) for g in range(GROUPS)]
        rdenom = two("rdenom", [P, 8])
        rdenom_own = two("rdenom_own", [P, 8, 4])
        heads_out = two("heads_out", [P, GROUPS * BLOCKS, W])
        r1 = two("r1", [P, 4, P])
        x1 = two("x1", [P, 4, P])
        x1_b2 = two("x1_b2", [P, 4, P])
        x_lnb = two("x_lnb", [P, 4, P])
        x1T = sb("x1T", [P, 4 * P])
        hidT = sb("hidT", [P, FC, 4 * P])
        r2 = sb("r2", [P, 4, P])
        y2 = sb("y2", [P, 4, P])
        x3 = two("x3", [P, 4, P + 1])
        stats = sb("stats", [P, 4, 6])
        moments = sb("moments", [P, 4, 2])
        var_eps = sb("var_eps", [P, 4])
        rstd = sb("rstd", [P, 4])
        cov = sb("cov", [P, P + 1])
        mean_row = sb("mean_row", [1, P])
        prod = sb("prod", [P, PH, P])
        q_mean = sb("q_mean", [P, PH])
        q_var = sb("q_var", [P, PH])
        q_rstd = sb("q_rstd", [P, PH])
        q_scale = sb("q_scale", [P, PH])
        q_shift = sb("q_shift", [P, PH])
        keys_scaled = sb("keys_scaled", [P, PH, KEYS])
        keys_shifted = sb("keys_shifted", [P, PH, KEYS])
        w_sim = sb("w_sim", [P, PH * KEYS])
        c_sim = sb("c_sim", [P, PH * KEYS])
        xT_tile = two("xT_tile", [P, P])
        sim = two("sim", [P, PH, KEYS])
        top = two("top", [P, PH, TOPK])
        top_rel = two("top_rel", [P, PH, TOPK])
        cand = prod[:, PK_HEADS:PK_HEADS + 4, :].rearrange("p a (b c d) -> p (a b) c d", b=2, c=TOPK)
        best = two("best", [P, PK_HEADS, TOPK])
        best_exp = two("best_exp", [P, PK_HEADS, TOPK])
        z = sb("z", [P, PK_HEADS])
        rz = two("rz", [P, PK_HEADS])
        minus_lnz = two("minus_lnz", [P, PK_HEADS])
        threshold = two("threshold", [P, PK_HEADS])
        sim_rel = sb("sim_rel", [P, PH, KEYS])
        parts = sb("parts", [P, PK_HEADS, 4, KEYS], F16)
        partsT = two("partsT", [P, PK_HEADS, P], F16)
        expgrid = [s[:].rearrange("p k c -> p (k c)")[:, 0:EXPERTS] for s in shifted]
        weights = [s[:].rearrange("p k c -> p (k c)")[:, 0:EXPERTS] for s in probs]
        act = [hidT[:, 2 * p:2 * p + 2, :].rearrange("p c i -> p (c i)") for p in range(2)]
        gated = prod[:, 0:EC, :]
        out_tile = two("out_tile", [P, P])
        res4 = sb("res4", [P, P])
        stats4 = sb("stats4", [P, 6])
        mom4 = sb("mom4", [P, 2])
        var4 = sb("var4", [P, 1])
        rstd4 = sb("rstd4", [P, 1])

        weights_in = sem("weights_in")
        ident_ready = sem("ident_ready")
        consts_ready = sem("consts_ready")
        band_ready = sem("band_ready")
        band_spread = sem("band_spread")
        mask_ready = sem("mask_ready")
        x4_in = two_sems("x4_in")
        a_transposed = sem("a_transposed")
        a_copied = sem("a_copied")
        v_in = two_sems("v_in")
        x_in = two_sems("x_in")
        operands_ready = sem("operands_ready")
        v_ready = sem("v_ready")
        scores_done = sem("scores_done")
        max_done = sem("max_done")
        shift_done = sem("shift_done")
        exp_done = sem("exp_done")
        pt_done = sem("pt_done")
        pt_copied = sem("pt_copied")
        pv_done = sem("pv_done")
        norm_step = sem("norm_step")
        norm_done = sem("norm_done")
        attn_done = sem("attn_done")
        r1_done = sem("r1_done")
        seq = sem("seq")
        r1_staged = sem("r1_staged")
        xlnb_ready = sem("xlnb_ready")
        stat_step = sem("stat_step")
        var_done = sem("var_done")
        rstd_done = sem("rstd_done")
        ln_step = sem("ln_step")
        x1_done = sem("x1_done")
        x1b2_done = sem("x1b2_done")
        x1T_done = sem("x1T_done")
        x1T_copied = sem("x1T_copied")
        ff1_done = sem("ff1_done")
        relu_done = sem("relu_done")
        ff2_done = sem("ff2_done")
        r2_done = sem("r2_done")
        x3_done = sem("x3_done")
        x3_kept = sem("x3_kept")
        x3T_done = sem("x3T_done")
        x3T_copied = sem("x3T_copied")
        gram_done = sem("gram_done")
        r2_normed = sem("r2_normed")
        r2_scaled = sem("r2_scaled")
        r2_summed = sem("r2_summed")
        c_var = sem("c_var")
        c_pe = sem("c_pe")
        c_dve = sem("c_dve")
        c_pool = sem("c_pool")
        xT_staged = sem("xT_staged")
        down_done = sem("down_done")
        gelu_done = sem("gelu_done")
        sim_done = sem("sim_done")
        sim_copied = sem("sim_copied")
        top_done = sem("top_done")
        top_step = sem("top_step")
        best_done = sem("best_done")
        bestexp_done = sem("bestexp_done")
        z_step = sem("z_step")
        rz_done = sem("rz_done")
        lnz_done = sem("lnz_done")
        part_step = sem("part_step")
        parts_done = sem("parts_done")
        partsT_done = sem("partsT_done")
        partsT_copied = sem("partsT_copied")
        grid_done = sem("grid_done")
        gridexp_done = sem("gridexp_done")
        weighed = sem("weighed")
        summed = sem("summed")
        gated_done = sem("gated_done")
        up_done = sem("up_done")
        res_done = sem("res_done")
        d_step = sem("d_step")
        d_var = sem("d_var")
        d_rstd = sem("d_rstd")
        out_ready = sem("out_ready")
        stored = two_sems("stored")

        N_WEIGHTS = 15
        block = ctx.enter_context(nc.Block())

        def need(eng, s, n):
            if not isinstance(n, int) or n > 0:
                eng.wait_ge(s, n)

        def hold(eng):
            eng.sem_inc(seq, 1)

        def over_pairs(eng, n, body):
            body(0, True, False)
            with eng.Fori(1, n - 1) as i:
                body(i, False, False)
            body(n - 1, False, True)

        def bcast(ap, dim, n):
            wide = ap.unsqueeze(dim)
            return wide.broadcast_to([n if d == dim else size for d, size in enumerate(wide.shape)])

        def stretch(ap, n):
            return ap.broadcast_to(list(ap.shape[:-1]) + [n])

        def tok(t, n=P):
            return bass.ds(t * P, n)

        @block.sync
        def _(sp):
            for q in range(2):
                sp.dma_start(x4[q][:], x[q * 512:(q + 1) * 512, :].rearrange("(a p) d -> p a d", p=P)).then_inc(x4_in[q], 16)
            row = lambda v: v.rearrange("(a d) -> a d", a=1).broadcast_to([P, P])
            for dst, src in (
                (ln1_g_all[:], row(ln1_g)), (ln1_b_all[:], row(ln1_b)), (ln2_g_all[:], row(ln2_g)),
                (ln2_b_all[:], row(ln2_b)), (b2_all[:], row(b2)),
                (b1_col[:], b1), (w1_sb[:], w1), (w2_sb[:], w2.rearrange("(c p) d -> p c d", p=P)),
                (wq_sb[:], w_q), (wqT_sb[:], w_qT), (keysT_sb[:], keysT), (gamma_sb[:], gamma), (beta_sb[:], beta),
                (downT_sb[:], downT), (up_sb[:], up.rearrange("(c p) d -> p c d", p=P)),
            ):
                sp.dma_start(dst, src).then_inc(weights_in, 16)
            with sp.Fori(1, NQ // 2) as i:
                for q in range(2):
                    sp.wait_ge(a_transposed, 2 * i + q - 1)
                    sp.dma_start(x4[q][:], x[bass.ds((2 * i + q) * 512, 512), :].rearrange("(a p) d -> p a d", p=P)
                                 ).then_inc(x4_in[q], 16)

            def b1_loads(i, first, last):
                for p in range(2):
                    t = 2 * i + p
                    need(sp, v_ready, t - 1)
                    for b in range(BLOCKS):
                        sp.dma_start(v_raw[p][:, b, :], x_wrapped[bass.ds(t * P + b * W, WIN), :]).then_inc(v_in[p], 16)
                    need(sp, r1_done, t - 1)
                    sp.dma_start(x_tile[p][:], x[tok(t), :]).then_inc(x_in[p], 16)
            over_pairs(sp, PAIRS, b1_loads)

            def b2_loads(i, first, last):
                for q in range(2):
                    n = 2 * i + q
                    if first:
                        sp.wait_ge(a_transposed, NQ)
                    need(sp, xlnb_ready, n - 1)
                    sp.dma_start(x4[q][:], x[bass.ds(n * 512, 512), :].rearrange("(a p) d -> p a d", p=P)
                                 ).then_inc(x4_in[q], 16)
            over_pairs(sp, NQ // 2, b2_loads)

            def stores(i, first, last):
                for p in range(2):
                    t = 2 * i + p
                    sp.wait_ge(out_ready, t + 1)
                    sp.dma_start(out[tok(t), :], out_tile[p][:]).then_inc(stored[p], 16)
            over_pairs(sp, PAIRS, stores)
            for p in range(2):
                sp.wait_ge(stored[p], 16 * PAIRS + 16)

        @block.gpsimd
        def _(pool):
            nc.gpsimd.memset(minus_half[:], -0.5)
            nc.gpsimd.memset(ones[:], 1.0)
            nc.gpsimd.memset(zeros[:], 0.0)
            nc.gpsimd.memset(xT[:, 0:W], 0.0)
            nc.gpsimd.memset(xT[:, W + tokens:W + tokens + W], 0.0)
            for q in range(2):
                nc.gpsimd.memset(v_ones[q][:], 1.0)
                nc.gpsimd.memset(x3[q][:], 1.0)
            nc.gpsimd.memset(band[:], 0.0)
            nc.gpsimd.memset(ident[:], 0.0).then_inc(ident_ready, 1)
            pool.wait_ge(ident_ready, 1)
            nc.gpsimd.affine_select(out=ident[:], in_=ident[:], compare_op=ALU.not_equal, fill=1.0, base=0,
                                    pattern=[[-1, P]], channel_multiplier=1).then_inc(ident_ready, 1)
            nc.gpsimd.affine_select(out=band[:], in_=band[:], compare_op=ALU.is_ge, fill=MASKED, base=0,
                                    pattern=[[1, WIN]], channel_multiplier=-1).then_inc(band_ready, 1)
            pool.wait_ge(band_ready, 1)
            nc.gpsimd.affine_select(out=band[:], in_=band[:], compare_op=ALU.is_ge, fill=MASKED, base=2 * W,
                                    pattern=[[-1, WIN]], channel_multiplier=1).then_inc(band_ready, 1)
            pool.wait_ge(consts_ready, 6)
            pool.wait_ge(a_copied, NQ)

            def b1_operands(i, first, last):
                for p in range(2):
                    t = 2 * i + p
                    need(pool, scores_done, GROUPS * (t - 1))
                    hold(pool)
                    nc.gpsimd.tensor_copy(window[p][:], xT[:, tok(t, P + 2 * W)]).then_inc(operands_ready, 1)
                    pool.wait_ge(operands_ready, 5 * t + 1)
                    hold(pool)
                    own = window[p][:, W:W + P].rearrange("p (b j) -> p b j", b=BLOCKS)
                    for h in range(4):
                        nc.gpsimd.tensor_scalar(queries[p][:, :, h, :], own, head_in_group[:, h:h + 1], None,
                                                ALU.mult).then_inc(operands_ready, 1)
                    need(pool, v_in[p], 16 * BLOCKS * (i + 1))
                    need(pool, pv_done, GROUPS * (t - 1))
                    hold(pool)
                    nc.gpsimd.tensor_copy(v_ones[p][:, :, :, 0:32].rearrange("p b g d -> p (b g) d"),
                                          v_raw[p][:].rearrange("p b (g d) -> p (b g) d", g=GROUPS)).then_inc(v_ready, 1)
            over_pairs(pool, PAIRS, b1_operands)

            pool.wait_ge(weights_in, 16 * N_WEIGHTS)

            def rsqrt(k):
                pool.wait_ge(var_done, k)
                hold(pool)
                nc.gpsimd.tensor_tensor(rstd[:], var_eps[:], minus_half[:, 0:4], ALU.pow).then_inc(rstd_done, 1)

            def stage_in(n, q, first_pair):
                pool.wait_ge(r1_done, 4 * n + 4)
                need(pool, x1_done, n - 1)
                hold(pool)
                nc.gpsimd.tensor_copy(r1[q][:].rearrange("p a d -> p (a d)"), kept[:, bass.ds(n * 512, 512)]
                                      ).then_inc(r1_staged, 1)

            def side_sums(n, i, q):
                pool.wait_ge(x4_in[q], 16 * (NQ // 2) + 16 * (i + 1))
                need(pool, x3_done, n - 1)
                hold(pool)
                nc.gpsimd.tensor_tensor(x_lnb[q][:], x4[q][:], bcast(ln2_b_all[:], 1, 4), ALU.add
                                        ).then_inc(xlnb_ready, 1)
                pool.wait_ge(x1_done, n + 1)
                need(pool, r2_done, n - 1)
                hold(pool)
                nc.gpsimd.tensor_tensor(x1_b2[q][:], x1[q][:], bcast(b2_all[:], 1, 4), ALU.add
                                        ).then_inc(x1b2_done, 1)

            stage_in(0, 0, True)
            rsqrt(1)

            def b2_pool(i, first, last):
                for q in range(2):
                    n = 2 * i + q
                    if not (last and q == 1):
                        stage_in(n + 1, 1 - q, first)
                        rsqrt(3 * n + 2)
                    side_sums(n, i, q)
                    end = 1 if last and q == 1 else 0
                    rsqrt(3 * n + 3 - end)
                    rsqrt(3 * n + 4 - end)
                    pool.wait_ge(x3_done, n + 1)
                    hold(pool)
                    nc.gpsimd.tensor_copy(kept[:, bass.ds(n * 512, 512)].rearrange("p (a d) -> p a d", a=4),
                                          x3[q][:, :, 0:P]).then_inc(x3_kept, 1)
            over_pairs(pool, NQ // 2, b2_pool)

            pool.wait_ge(c_dve, 5)
            hold(pool)
            nc.gpsimd.tensor_tensor(q_rstd[:], q_var[:], minus_half[:, 0:PH], ALU.pow).then_inc(c_pool, 1)

            pool.wait_ge(x3T_copied, NQ)

            def stage_x(t, p):
                need(pool, sim_done, t - 1)
                hold(pool)
                nc.gpsimd.tensor_copy(xT_tile[p][:], xT[:, tok(t)]).then_inc(xT_staged, 1)

            def split(t, p):
                pool.wait_ge(top_done, t + 1)
                hold(pool)
                nc.gpsimd.tensor_tensor(sim_rel[:], sim[p][:], stretch(top[p][:, :, 0:1], KEYS), ALU.subtract
                                        ).then_inc(part_step, 1)
                pool.wait_ge(part_step, 3 * t + 1)
                hold(pool)
                nc.gpsimd.tensor_scalar(sim_rel[:], sim_rel[:], FAR, None, ALU.max).then_inc(part_step, 1)
                pool.wait_ge(part_step, 3 * t + 2)
                need(pool, partsT_done, t)
                hold(pool)
                view = parts[:].rearrange("p h (a b) k -> p a b h k", a=2)
                rel = sim_rel[:].rearrange("p (a h) k -> p a h k", a=2)
                nc.gpsimd.tensor_copy(view[:, :, 0], rel).then_inc(part_step, 1)
                pool.wait_ge(part_step, 3 * t + 3)
                hold(pool)
                nc.gpsimd.tensor_tensor(view[:, :, 1], rel, view[:, :, 0], ALU.subtract).then_inc(parts_done, 1)

            stage_x(0, 0)
            split(0, 0)

            def d_pool(i, first, last):
                for p in range(2):
                    t = 2 * i + p
                    if not (first and p == 0):
                        pool.wait_ge(d_var, t)
                        hold(pool)
                        nc.gpsimd.tensor_tensor(rstd4[:], var4[:], minus_half[:, 0:1], ALU.pow).then_inc(d_rstd, 1)
                    if not (last and p == 1):
                        stage_x(t + 1, 1 - p)
                        split(t + 1, 1 - p)
            over_pairs(pool, PAIRS, d_pool)
            pool.wait_ge(d_var, NT)
            hold(pool)
            nc.gpsimd.tensor_tensor(rstd4[:], var4[:], minus_half[:, 0:1], ALU.pow).then_inc(d_rstd, 1)

        @block.tensor
        def _(pe):
            pe.wait_ge(ident_ready, 2)

            def a_transpose(i, first, last):
                for q in range(2):
                    n = 2 * i + q
                    pe.wait_ge(x4_in[q], 16 * (i + 1))
                    need(pe, a_copied, n - 1)
                    for a in range(4):
                        mm = nc.tensor.transpose(ps[:, q, a * P:(a + 1) * P], x4[q][:, a, :], ident[:])
                    mm.then_inc(a_transposed, 1)
            over_pairs(pe, NQ // 2, a_transpose)

            pe.wait_ge(consts_ready, 6)
            pe.wait_ge(band_ready, 2)
            nc.tensor.matmul(ps[:, 2, 0:WIN], spread4[:], band[:], start=True, stop=True).then_inc(band_spread, 1)
            pe.wait_ge(mask_ready, 3)

            def scores(t, p, mask_at):
                pe.wait_ge(operands_ready, 5 * (t + 1))
                for g in range(GROUPS):
                    if g % 2 == 0:
                        need(pe, shift_done, 2 * (t - 1) + g // 2 + 1)
                        if isinstance(t, int) and t == 0:
                            pe.wait_ge(a_copied, NQ)
                    nc.tensor.matmul(ps[:, g, 0:BLOCKS * WIN], ident_bf[:], mask[:, mask_at], start=True, stop=False,
                                     skip_group_check=True)
                for b in range(BLOCKS):
                    for g in range(GROUPS):
                        rows = slice(32 * g, 32 * g + 32)
                        mm = nc.tensor.matmul(ps[:, g, b * WIN:(b + 1) * WIN], queries[p][rows, b],
                                              window[p][rows, b * W:b * W + WIN], start=False, stop=True,
                                              skip_group_check=True)
                        if b == BLOCKS - 1:
                            mm.then_inc(scores_done, 1)

            def probs_transpose(t, p):
                for g in range(GROUPS):
                    pe.wait_ge(exp_done, 2 * t + g // 2 + 1)
                    need(pe, pt_copied, GROUPS * t + g - 1)
                    if g == 0:
                        need(pe, r1_done, t - 1)
                    for b in range(BLOCKS):
                        mm = nc.tensor.transpose(ps[0:WIN, 4 + g % 2, b * P:(b + 1) * P],
                                                 probs[p][:, g * BLOCKS + b, :], ident[:])
                    mm.then_inc(pt_done, 1)

            def values(t, p):
                pe.wait_ge(v_ready, t + 1)
                for g in range(GROUPS):
                    pe.wait_ge(pt_copied, GROUPS * t + g + 1)
                    if g % 2 == 0:
                        need(pe, norm_done, 2 * (t - 1) + g // 2 + 1)
                    for b in range(BLOCKS):
                        k = (g % 2) * BLOCKS + b
                        mm = nc.tensor.matmul(ps[:, 6 + g // 2, k * VW:(k + 1) * VW], probsT[g][:, b, :],
                                              v_ones[p][:, b, g, :], start=True, stop=True)
                    mm.then_inc(pv_done, 1)

            def attn_out(t, p, copied):
                pe.wait_ge(norm_done, 2 * t + 2)
                pe.wait_ge(pt_copied, copied)
                view = heads_out[p][:].rearrange("p (g b) c -> p b g c", g=GROUPS)
                for b in range(BLOCKS):
                    mm = nc.tensor.matmul(ps[32 * b:32 * b + 32, 4, 0:P], fold4[:], view[:, b], start=True, stop=True)
                mm.then_inc(attn_done, 1)

            def mask_of(r):
                return bass.ds(r * BLOCKS * WIN, BLOCKS * WIN)

            def b1_tile(t, p, r_next, first, last):
                probs_transpose(t, p)
                if not (first and p == 0):
                    attn_out(t - 1, 1 - p, GROUPS * t + 3)
                if not (last and p == 1):
                    scores(t + 1, 1 - p, mask_of(r_next))
                values(t, p)

            scores(0, 0, mask_of(0))
            BP = TB // 2
            for p in range(2):
                b1_tile(p, p, p + 1, True, False)
            with pe.Fori(1, BP) as j:
                b1_tile(2 * j, 0, 2 * j + 1, False, False)
                b1_tile(2 * j + 1, 1, (2 * j + 2) % TB, False, False)
            with pe.Fori(1, NT // TB - 1) as s:
                with pe.Fori(0, BP) as j:
                    b1_tile(s * TB + 2 * j, 0, 2 * j + 1, False, False)
                    b1_tile(s * TB + 2 * j + 1, 1, (2 * j + 2) % TB, False, False)
            with pe.Fori(0, BP - 1) as j:
                b1_tile(NT - TB + 2 * j, 0, 2 * j + 1, False, False)
                b1_tile(NT - TB + 2 * j + 1, 1, 2 * j + 2, False, False)
            for p in range(2):
                b1_tile(NT - 2 + p, p, TB - 1, False, True)
            attn_out(NT - 1, 1, GROUPS * NT)

            pe.wait_ge(weights_in, 16 * N_WEIGHTS)
            pe.wait_ge(shift_done, 2 * NT)
            pe.wait_ge(r1_done, NT)
            pe.wait_ge(norm_done, 2 * NT)
            nc.tensor.matmul(ps[:, 5, 0:P + 1], ident_bf[:], zeros[:], start=True, stop=False,
                             skip_group_check=True)

            def feed_forward(n, q):
                pe.wait_ge(x1_done, n + 1)
                need(pe, x1T_copied, n)
                for a in range(4):
                    mm = nc.tensor.transpose(ps[:, 0, a * P:(a + 1) * P], x1[q][:, a, :], ident[:])
                mm.then_inc(x1T_done, 1)
                pe.wait_ge(x1T_copied, n + 1)
                for c in range(FC):
                    need(pe, relu_done, FC * n + c - 1)
                    nc.tensor.matmul(ps[:, 1 + c % 2, :], w1_sb[:, c * P:(c + 1) * P], x1T[:], start=True, stop=True
                                     ).then_inc(ff1_done, 1)
                pe.wait_ge(relu_done, FC * (n + 1))
                need(pe, r2_done, n)
                for a in range(4):
                    for c in range(FC):
                        mm = nc.tensor.matmul(ps[:, 3, a * P:(a + 1) * P], hidT[:, c, a * P:(a + 1) * P],
                                              w2_sb[:, c, :], start=(c == 0), stop=(c == FC - 1))
                mm.then_inc(ff2_done, 1)

            def result_products(n, q):
                pe.wait_ge(x3_done, n + 1)
                need(pe, x3T_copied, n)
                for a in range(4):
                    mm = nc.tensor.transpose(ps[:, 4, a * P:(a + 1) * P], x3[q][:, a, 0:P], ident[:])
                mm.then_inc(x3T_done, 1)
                for a in range(4):
                    mm = nc.tensor.matmul(ps[:, 5, 0:P + 1], x3[q][:, a, 0:P], x3[q][:, a, :], start=False, stop=True,
                                          skip_group_check=True)
                mm.then_inc(gram_done, 1)

            feed_forward(0, 0)

            def b2_pe(i, first, last):
                for q in range(2):
                    if not (last and q == 1):
                        feed_forward(2 * i + q + 1, 1 - q)
                    result_products(2 * i + q, q)
            over_pairs(pe, NQ // 2, b2_pe)

            pe.wait_ge(c_dve, 1)
            nc.tensor.matmul(ps[0:1, 6, 0:P], cov[:, P:P + 1], ident[:], start=True, stop=True).then_inc(c_pe, 1)
            pe.wait_ge(c_dve, 2)
            nc.tensor.matmul(ps[:, 7, 0:P], mean_row[:], mean_row[:], start=True, stop=True).then_inc(c_pe, 1)
            pe.wait_ge(c_dve, 3)
            pe.wait_ge(x3T_copied, NQ)
            for k in range(PH):
                mm = nc.tensor.matmul(ps[:, k // 3, (k % 3) * (P + 1):(k % 3 + 1) * (P + 1)],
                                      wq_sb[:, k * P:(k + 1) * P], cov[:], start=True, stop=True)
            mm.then_inc(c_pe, 1)
            pe.wait_ge(c_dve, 8)
            for k in range(PH):
                nc.tensor.matmul(ps[:, 6, k * KEYS:(k + 1) * KEYS], wqT_sb[:, k, :], keys_scaled[:, k, :],
                                 start=True, stop=True)
            nc.tensor.matmul(ps[:, 7, :], ones[:], keys_shifted[:].rearrange("p a k -> p (a k)"), start=True, stop=True
                             ).then_inc(c_pe, 1)
            pe.wait_ge(c_dve, 10)

            def down(t, p):
                pe.wait_ge(xT_staged, t + 1)
                need(pe, res_done, t - 1)
                need(pe, partsT_copied, t)
                for c in range(EC):
                    mm = nc.tensor.matmul(ps[:, 6 + c // 4, (c % 4) * P:(c % 4 + 1) * P], downT_sb[:, c * P:(c + 1) * P],
                                          xT_tile[p][:], start=True, stop=True)
                    if c % 4 == 3:
                        mm.then_inc(down_done, 1)

            def similarities(t, p):
                pe.wait_ge(gelu_done, 2 * t + 1)
                nc.tensor.matmul(ps[:, 6, :], xT_tile[p][:], w_sim[:], start=True, stop=True).then_inc(sim_done, 1)

            def parts_transpose(t, p):
                pe.wait_ge(parts_done, t + 1)
                pe.wait_ge(gelu_done, 2 * t + 2)
                bank = ps[:, 7, :].bitcast(F16)
                for h in range(PK_HEADS):
                    mm = nc.tensor.transpose(bank[:, h * P:(h + 1) * P], parts[:, h].rearrange("p a k -> p (a k)"),
                                             ident_h[:])
                mm.then_inc(partsT_done, 1)

            def grid(t, p, h):
                if h == 0:
                    pe.wait_ge(partsT_copied, t + 1)
                need(pe, weighed, PK_HEADS * t + h - 1)
                for half in range(2):
                    mm = nc.tensor.matmul(ps[:, 2 * (h % 2) + half, :], partsT[p][:, h, :],
                                          spread_keys[:, half * 512:(half + 1) * 512], start=True, stop=True)
                mm.then_inc(grid_done, 1)

            def sum_heads(t, h):
                pe.wait_ge(weighed, PK_HEADS * t + h + 1)
                if h == 0:
                    need(pe, gated_done, t)
                for c in range(EC):
                    mm = nc.tensor.matmul(ps[:, 4 + c // 4, (c % 4) * P:(c % 4 + 1) * P],
                                          weights[h % 2][:, c * P:(c + 1) * P], ident[:], is_transpose=True,
                                          start=(h == 0 and c % 4 == 0), stop=(h == PK_HEADS - 1),
                                          skip_group_check=True)
                mm.then_inc(summed, 1)

            def up_projection(t):
                pe.wait_ge(gated_done, t + 1)
                pe.wait_ge(sim_copied, t + 2 if not (isinstance(t, int) and t == NT - 1) else NT)
                for c in range(EC):
                    mm = nc.tensor.matmul(ps[:, 6, 0:P], gated[:, c, :], up_sb[:, c, :], start=(c == 0),
                                          stop=(c == EC - 1))
                mm.then_inc(up_done, 1)

            down(0, 0)
            similarities(0, 0)
            parts_transpose(0, 0)

            def d_pe(i, first, last):
                for p in range(2):
                    t = 2 * i + p
                    more = not (last and p == 1)
                    grid(t, p, 0)
                    grid(t, p, 1)
                    if not (first and p == 0):
                        up_projection(t - 1)
                    sum_heads(t, 0)
                    grid(t, p, 2)
                    if more:
                        down(t + 1, 1 - p)
                    sum_heads(t, 1)
                    grid(t, p, 3)
                    if more:
                        similarities(t + 1, 1 - p)
                    for h in range(2, 6):
                        sum_heads(t, h)
                        grid(t, p, h + 2)
                    sum_heads(t, 6)
                    if more:
                        parts_transpose(t + 1, 1 - p)
                    sum_heads(t, 7)
            over_pairs(pe, PAIRS, d_pe)
            up_projection(NT - 1)

        @block.scalar
        def _(a):
            def copy(out_ap, in_ap):
                return nc.scalar.activation(out_ap, in_ap, ACT.Copy)

            def a_copy(i, first, last):
                for q in range(2):
                    n = 2 * i + q
                    a.wait_ge(a_transposed, n + 1)
                    copy(xT[:, bass.ds(W + n * 512, 512)], ps[:, q, :]).then_inc(a_copied, 1)
            over_pairs(a, NQ // 2, a_copy)

            def exps(t, p):
                for half in range(2):
                    a.wait_ge(shift_done, 2 * t + half + 1)
                    need(a, pt_done, GROUPS * (t - 2) + 2 * half + 2)
                    s = slice(8 * half, 8 * half + 8)
                    nc.scalar.activation(probs[p][:, s, :], shifted[p][:, s, :], ACT.Exp).then_inc(exp_done, 1)

            def probs_copy(t):
                for g in range(GROUPS):
                    a.wait_ge(pt_done, GROUPS * t + g + 1)
                    need(a, pv_done, GROUPS * (t - 1) + g + 1)
                    copy(probsT[g][:].rearrange("p b i -> p (b i)"), ps[0:WIN, 4 + g % 2, :]).then_inc(pt_copied, 1)

            exps(0, 0)

            def b1_act(i, first, last):
                for p in range(2):
                    probs_copy(2 * i + p)
                    if not (last and p == 1):
                        exps(2 * i + p + 1, 1 - p)
            over_pairs(a, PAIRS, b1_act)

            a.wait_ge(weights_in, 16 * N_WEIGHTS)

            def hidden(n):
                a.wait_ge(x1T_done, n + 1)
                need(a, ff1_done, FC * n)
                copy(x1T[:], ps[:, 0, :]).then_inc(x1T_copied, 1)
                need(a, ff2_done, n)
                for c in range(FC):
                    a.wait_ge(ff1_done, FC * n + c + 1)
                    nc.scalar.activation(hidT[:, c, :], ps[:, 1 + c % 2, :], ACT.Relu, bias=b1_col[:, c:c + 1]
                                         ).then_inc(relu_done, 1)

            def result_copy(n):
                a.wait_ge(x3T_done, n + 1)
                copy(xT[:, bass.ds(n * 512, 512)], ps[:, 4, :]).then_inc(x3T_copied, 1)

            hidden(0)

            def b2_act(i, first, last):
                for q in range(2):
                    if not (last and q == 1):
                        hidden(2 * i + q + 1)
                    result_copy(2 * i + q)
            over_pairs(a, NQ // 2, b2_act)

            def gelus(t, p):
                need(a, gated_done, t - 1)
                for half in range(2):
                    a.wait_ge(down_done, 2 * t + half + 1)
                    nc.scalar.activation(act[p][:, half * 512:(half + 1) * 512], ps[:, 6 + half, :],
                                         ACT.Gelu_apprx_tanh).then_inc(gelu_done, 1)

            def best_exps(t, p):
                a.wait_ge(best_done, t + 1)
                nc.scalar.activation(best_exp[p][:], best[p][:], ACT.Exp).then_inc(bestexp_done, 1)

            def log_z(t, p):
                a.wait_ge(rz_done, t + 1)
                nc.scalar.activation(minus_lnz[p][:], rz[p][:], ACT.Ln).then_inc(lnz_done, 1)

            def parts_copy(t, p):
                a.wait_ge(partsT_done, t + 1)
                copy(partsT[p][:].rearrange("p h i -> p (h i)"), ps[:, 7, :].bitcast(F16)).then_inc(partsT_copied, 1)

            def grid_exp(t, p, h):
                a.wait_ge(grid_done, PK_HEADS * t + h + 1)
                need(a, weighed, PK_HEADS * t + h - 1)
                if h == 0:
                    a.wait_ge(lnz_done, t + 1)
                nc.scalar.activation(expgrid[h % 2], ps[:, 2 * (h % 2):2 * (h % 2) + 2, :].rearrange("p a b -> p (a b)"),
                                     ACT.Exp, bias=minus_lnz[p][:, h:h + 1]).then_inc(gridexp_done, 1)

            gelus(0, 0)
            best_exps(0, 0)
            log_z(0, 0)
            parts_copy(0, 0)

            def d_act(i, first, last):
                for p in range(2):
                    t = 2 * i + p
                    more = not (last and p == 1)
                    for h in range(3):
                        grid_exp(t, p, h)
                    if more:
                        gelus(t + 1, 1 - p)
                    for h in range(3, 6):
                        grid_exp(t, p, h)
                    if more:
                        best_exps(t + 1, 1 - p)
                    for h in range(6, 8):
                        grid_exp(t, p, h)
                    if more:
                        log_z(t + 1, 1 - p)
                        parts_copy(t + 1, 1 - p)
            over_pairs(a, PAIRS, d_act)

        @block.vector
        def _(v):
            V = nc.vector
            for p in range(2):
                v.sem_inc(stored[p], 16)
            v.wait_ge(ident_ready, 2)
            V.tensor_reduce(fold4[:], ident[:].rearrange("p (q c) -> p c q", q=4), AX_X, ALU.add).then_inc(consts_ready, 1)
            V.tensor_reduce(quadrant[:], ident[:].rearrange("p (q c) -> p q c", q=4), AX_X, ALU.add
                            ).then_inc(consts_ready, 1)
            V.tensor_reduce(head16[:], ident[:].rearrange("p (h e) -> p h e", e=DH), AX_X, ALU.add
                            ).then_inc(consts_ready, 1)
            V.tensor_copy(spread4[:].rearrange("p (q c) -> p q c", q=4), bcast(ident[0:W, 0:W], 1, 4)
                          ).then_inc(consts_ready, 1)
            V.tensor_copy(ident_bf[:], ident[:]).then_inc(consts_ready, 1)
            v.wait_ge(consts_ready, 5)
            V.tensor_reduce(head_in_group[:], head16[:].rearrange("p (q h) -> p h q", q=4), AX_X, ALU.add
                            ).then_inc(consts_ready, 1)
            V.tensor_copy(ident_h[:], ident[:])
            for q in range(4):
                rows = slice(32 * q, 32 * q + 32)
                one = ident[rows, 32 * q:32 * q + 32]
                V.tensor_copy(spread_keys[rows, :].rearrange("p (i j) -> p i j", i=KEYS),
                              bcast(one, 2, KEYS) if q < 2 else bcast(one, 1, KEYS))
            v.wait_ge(band_spread, 1)
            m = mask[:].rearrange("p (b c) -> p b c", c=WIN)
            V.tensor_copy(m, bcast(ps[:, 2, 0:WIN], 1, TB * BLOCKS)).then_inc(mask_ready, 1)
            v.wait_ge(mask_ready, 1)
            V.memset(m[:, 0, 0:W], MASKED).then_inc(mask_ready, 1)
            V.memset(m[:, TB * BLOCKS - 1, 2 * W:WIN], MASKED).then_inc(mask_ready, 1)

            def shift(t, p):
                for half in range(2):
                    at = 8 * half
                    sc = ps[:, 2 * half:2 * half + 2, 0:BLOCKS * WIN].rearrange("p a (b c) -> p a b c", c=WIN)
                    mx = row_max[p][:, at:at + 8]
                    v.wait_ge(scores_done, GROUPS * t + 2 * half + 2)
                    V.tensor_reduce(mx.rearrange("p (a b) -> p a b", a=2), sc, AX_X, ALU.max).then_inc(max_done, 1)
                    v.wait_ge(max_done, 2 * t + half + 1)
                    need(v, exp_done, 2 * (t - 2) + half + 1)
                    V.tensor_tensor(shifted[p][:, at:at + 8, :].rearrange("p (a b) c -> p a b c", a=2), sc,
                                    bcast(mx.rearrange("p (a b) -> p a b", a=2), 3, WIN), ALU.subtract
                                    ).then_inc(shift_done, 1)

            def normalise(t, p):
                for half in range(2):
                    pv = ps[:, 6 + half, 0:8 * VW].rearrange("p (k c) -> p k c", c=VW)
                    n = 2 * t + half
                    v.wait_ge(pv_done, GROUPS * t + 2 * half + 2)
                    V.reciprocal(rdenom[half][:], pv[:, :, 32]).then_inc(norm_step, 1)
                    v.wait_ge(norm_step, 2 * n + 1)
                    V.tensor_tensor(rdenom_own[half][:], bcast(rdenom[half][:], 2, 4), bcast(quadrant[:], 1, 8), ALU.mult
                                    ).then_inc(norm_step, 1)
                    v.wait_ge(norm_step, 2 * n + 2)
                    if half == 0:
                        need(v, attn_done, t - 1)
                    V.tensor_tensor(heads_out[p][:, 8 * half:8 * half + 8, :].rearrange("p k (h d) -> p k h d", h=4),
                                    pv[:, :, 0:32].rearrange("p k (h d) -> p k h d", h=4),
                                    bcast(rdenom_own[half][:], 3, DH), ALU.mult).then_inc(norm_done, 1)

            def residual(t, i, p):
                v.wait_ge(attn_done, t + 1)
                v.wait_ge(x_in[p], 16 * (i + 1))
                V.tensor_tensor(kept[:, tok(t)], ps[:, 4, 0:P], x_tile[p][:], ALU.add).then_inc(r1_done, 1)

            shift(0, 0)

            def b1_dve(i, first, last):
                for p in range(2):
                    t = 2 * i + p
                    if not (first and p == 0):
                        residual(t - 1, i if p == 1 else i - 1, 1 - p)
                    if not (last and p == 1):
                        shift(t + 1, 1 - p)
                    normalise(t, p)
            over_pairs(v, PAIRS, b1_dve)
            residual(NT - 1, PAIRS - 1, 1)

            v.wait_ge(weights_in, 16 * N_WEIGHTS)

            def layernorm(k, src, dst, chain):
                for a in range(4):
                    V.bn_stats(stats[:, a, :], src[:, a, :]).then_inc(stat_step, 1)
                v.wait_ge(stat_step, 8 * k - 4)
                hold(v)
                for a in range(4):
                    V.bn_aggr(moments[:, a, :], stats[:, a, :]).then_inc(stat_step, 1)
                v.wait_ge(stat_step, 8 * k)
                V.tensor_scalar(var_eps[:], moments[:, :, 1], EPS, None, ALU.add).then_inc(var_done, 1)
                v.wait_ge(rstd_done, k)
                for a in range(4):
                    last = V.tensor_scalar(dst[:, a, :], src[:, a, :], moments[:, a, 0:1], rstd[:, a:a + 1],
                                           ALU.subtract, ALU.mult)
                last.then_inc(chain, 1)

            def ln1(n, q, k):
                v.wait_ge(r1_staged, n + 1)
                layernorm(k, r1[q], y2, ln_step)
                v.wait_ge(ln_step, 2 * n + 1)
                V.tensor_tensor(y2[:], y2[:], bcast(ln1_g_all[:], 1, 4), ALU.mult).then_inc(ln_step, 1)
                v.wait_ge(ln_step, 2 * n + 2)
                need(v, x1b2_done, n - 1)
                need(v, x1T_done, n - 1)
                V.tensor_tensor(x1[q][:], y2[:], bcast(ln1_b_all[:], 1, 4), ALU.add).then_inc(x1_done, 1)

            def ln23(n, q, k):
                v.wait_ge(ff2_done, n + 1)
                v.wait_ge(x1b2_done, n + 1)
                V.tensor_tensor(r2[:], ps[:, 3, :].rearrange("p (a d) -> p a d", a=4), x1_b2[q][:], ALU.add
                                ).then_inc(r2_done, 1)
                v.wait_ge(r2_done, n + 1)
                layernorm(k, r2, r2, r2_normed)
                v.wait_ge(r2_normed, n + 1)
                V.tensor_tensor(r2[:], r2[:], bcast(ln2_g_all[:], 1, 4), ALU.mult).then_inc(r2_scaled, 1)
                v.wait_ge(r2_scaled, n + 1)
                v.wait_ge(xlnb_ready, n + 1)
                V.tensor_tensor(r2[:], r2[:], x_lnb[q][:], ALU.add).then_inc(r2_summed, 1)
                v.wait_ge(r2_summed, n + 1)
                need(v, gram_done, n - 1)
                need(v, x3_kept, n - 1)
                layernorm(k + 1, r2, x3[q][:, :, 0:P], x3_done)

            ln1(0, 0, 1)

            def b2_dve(i, first, last):
                for q in range(2):
                    n = 2 * i + q
                    end = 1 if last and q == 1 else 0
                    if not end:
                        ln1(n + 1, 1 - q, 3 * n + 2)
                    ln23(n, q, 3 * n + 3 - end)
            over_pairs(v, NQ // 2, b2_dve)

            v.wait_ge(gram_done, NQ)
            V.tensor_scalar(cov[:], ps[:, 5, 0:P + 1], 1.0 / tokens, None, ALU.mult).then_inc(c_dve, 1)
            v.wait_ge(c_pe, 1)
            V.tensor_copy(mean_row[:], ps[0:1, 6, 0:P]).then_inc(c_dve, 1)
            v.wait_ge(c_pe, 2)
            V.scalar_tensor_tensor(cov[:, 0:P], ps[:, 7, 0:P], -1.0, cov[:, 0:P], ALU.mult, ALU.add).then_inc(c_dve, 1)
            v.wait_ge(c_pe, 3)
            for b in range(6):
                n = min(3, PH - 3 * b)
                z3 = ps[:, b, 0:n * (P + 1)].rearrange("p (k c) -> p k c", c=P + 1)
                V.tensor_tensor(prod[:, 3 * b:3 * b + n, :], z3[:, :, 0:P], wqT_sb[:, 3 * b:3 * b + n, :], ALU.mult)
                last = V.tensor_copy(q_mean[:, 3 * b:3 * b + n], z3[:, :, P])
            last.then_inc(c_dve, 1)
            v.wait_ge(c_dve, 4)
            V.tensor_reduce(q_var[:], prod[:], AX_X, ALU.add).then_inc(c_var, 1)
            v.wait_ge(c_var, 1)
            V.tensor_scalar(q_var[:], q_var[:], EPS, None, ALU.add).then_inc(c_dve, 1)
            v.wait_ge(c_pool, 1)
            V.tensor_tensor(q_scale[:], q_rstd[:], gamma_sb[:], ALU.mult).then_inc(c_var, 1)
            v.wait_ge(c_var, 2)
            V.tensor_tensor(q_shift[:], q_mean[:], q_scale[:], ALU.mult).then_inc(c_var, 1)
            v.wait_ge(c_var, 3)
            V.tensor_tensor(q_shift[:], beta_sb[:], q_shift[:], ALU.subtract).then_inc(c_dve, 1)
            v.wait_ge(c_dve, 6)
            V.tensor_tensor(keys_scaled[:], keysT_sb[:], bcast(q_scale[:], 2, KEYS), ALU.mult).then_inc(c_dve, 1)
            V.tensor_tensor(keys_shifted[:], keysT_sb[:], bcast(q_shift[:], 2, KEYS), ALU.mult).then_inc(c_dve, 1)
            v.wait_ge(c_pe, 4)
            V.tensor_copy(w_sim[:], ps[:, 6, :]).then_inc(c_dve, 1)
            V.tensor_copy(c_sim[:], ps[:, 7, :]).then_inc(c_dve, 1)
            v.wait_ge(c_dve, 10)

            def top_keys(t, p):
                v.wait_ge(sim_done, t + 1)
                need(v, part_step, 3 * (t - 2) + 1)
                V.tensor_tensor(sim[p][:].rearrange("p a k -> p (a k)"), ps[:, 6, :], c_sim[:], ALU.add
                                ).then_inc(sim_copied, 1)
                v.wait_ge(sim_copied, t + 1)
                hold(v)
                for k in range(PH):
                    last = V.max(top[p][:, k, :], sim[p][:, k, :])
                last.then_inc(top_done, 1)

            def top_pairs(t, p):
                v.wait_ge(top_done, t + 1)
                V.tensor_tensor(top_rel[p][:], top[p][:], stretch(top[p][:, :, 0:1], TOPK), ALU.subtract
                                ).then_inc(top_step, 1)
                v.wait_ge(top_step, 3 * t + 1)
                V.tensor_tensor(cand, bcast(top_rel[p][:, 0:PK_HEADS, :], 3, TOPK),
                                bcast(top_rel[p][:, PK_HEADS:PH, :], 2, TOPK), ALU.add).then_inc(top_step, 1)
                v.wait_ge(top_step, 3 * t + 2)
                hold(v)
                for h in range(PK_HEADS):
                    last = V.max(best[p][:, h, :], cand[:, h].rearrange("p a b -> p (a b)"))
                last.then_inc(best_done, 1)
                v.wait_ge(best_done, t + 1)
                V.tensor_scalar(threshold[p][:], best[p][:, :, TOPK - 1], 1.0 + SLACK, -SLACK, ALU.mult, ALU.add
                                ).then_inc(top_step, 1)

            def normaliser(t, p):
                v.wait_ge(bestexp_done, t + 1)
                V.tensor_reduce(z[:], best_exp[p][:], AX_X, ALU.add).then_inc(z_step, 1)
                v.wait_ge(z_step, t + 1)
                V.reciprocal(rz[p][:], z[:]).then_inc(rz_done, 1)

            def weigh(t, p, h):
                v.wait_ge(gridexp_done, PK_HEADS * t + h + 1)
                need(v, summed, PK_HEADS * t + h - 1)
                if h == 0:
                    v.wait_ge(top_step, 3 * t + 3)
                V.scalar_tensor_tensor(weights[h % 2], ps[:, 2 * (h % 2):2 * (h % 2) + 2, :].rearrange("p a b -> p (a b)"),
                                       threshold[p][:, h:h + 1], expgrid[h % 2], ALU.is_ge, ALU.mult
                                       ).then_inc(weighed, 1)

            def gate(t, p):
                v.wait_ge(summed, PK_HEADS * (t + 1))
                v.wait_ge(gelu_done, 2 * t + 2)
                need(v, up_done, t)
                V.tensor_tensor(gated.rearrange("p c i -> p (c i)"), ps[:, 4:6, :].rearrange("p a b -> p (a b)"),
                                act[p], ALU.mult).then_inc(gated_done, 1)

            def last_moments(t):
                v.wait_ge(up_done, t + 1)
                V.tensor_tensor(res4[:], ps[:, 6, 0:P], kept[:, tok(t)], ALU.add).then_inc(res_done, 1)
                v.wait_ge(res_done, t + 1)
                V.bn_stats(stats4[:], res4[:]).then_inc(d_step, 1)
                v.wait_ge(d_step, 2 * t + 1)
                hold(v)
                V.bn_aggr(mom4[:], stats4[:]).then_inc(d_step, 1)
                v.wait_ge(d_step, 2 * t + 2)
                V.tensor_scalar(var4[:], mom4[:, 1:2], EPS, None, ALU.add).then_inc(d_var, 1)

            def last_norm(t, i, p):
                v.wait_ge(d_rstd, t + 1)
                v.wait_ge(stored[p], 16 * i + 16)
                V.tensor_scalar(out_tile[p][:], res4[:], mom4[:, 0:1], rstd4[:], ALU.subtract, ALU.mult
                                ).then_inc(out_ready, 1)

            v.wait_ge(x3_kept, NQ)
            top_keys(0, 0)
            top_pairs(0, 0)
            normaliser(0, 0)

            def d_dve(i, first, last):
                for p in range(2):
                    t = 2 * i + p
                    more = not (last and p == 1)
                    before = not (first and p == 0)
                    weigh(t, p, 0)
                    if before:
                        last_moments(t - 1)
                    weigh(t, p, 1)
                    if before:
                        last_norm(t - 1, i if p == 1 else i - 1, 1 - p)
                    weigh(t, p, 2)
                    if more:
                        top_keys(t + 1, 1 - p)
                    weigh(t, p, 3)
                    if more:
                        top_pairs(t + 1, 1 - p)
                    weigh(t, p, 4)
                    weigh(t, p, 5)
                    weigh(t, p, 6)
                    if more:
                        normaliser(t + 1, 1 - p)
                    weigh(t, p, 7)
                    gate(t, p)
            over_pairs(v, PAIRS, d_dve)
            last_moments(NT - 1)
            last_norm(NT - 1, PAIRS - 1, 1)


_OUT = ((4, 1024, 128), "float32")


def kernel(**inputs):
    import numpy as np
    import concourse.bacc as bacc
    from concourse.bass_utils import run_bass_kernel_spmd

    a = {k: np.asarray(v) for k, v in inputs.items()}
    x = a["L0_attn_src"].reshape(4096, 128)
    arrays = {
        "x": x,
        "x_wrapped": np.concatenate([x[-W:], x, x[:W]]),
        "ln1_g": a["L0_attn_ln1_g"], "ln1_b": a["L0_attn_ln1_b"],
        "ln2_g": a["L0_attn_ln2_g"], "ln2_b": a["L0_attn_ln2_b"],
        "w1": a["L0_attn_W1"], "b1": a["L0_attn_b1"].reshape(FC, P).T,
        "w2": a["L0_attn_W2"], "b2": a["L0_attn_b2"],
        "w_q": a["L0_ffn_w_q"], "w_qT": a["L0_ffn_w_q"].reshape(P, PH, P).transpose(2, 1, 0),
        "gamma": a["L0_ffn_bn_gamma"].reshape(PH, P).T, "beta": a["L0_ffn_bn_beta"].reshape(PH, P).T,
        "keysT": a["L0_ffn_keys"].transpose(3, 2, 0, 1).reshape(P, PH, KEYS),
        "downT": a["L0_ffn_down_embed"].T, "up": a["L0_ffn_up_embed"],
    }
    arrays = {f"in_{k}": np.ascontiguousarray(v) for k, v in arrays.items()}
    nc = bacc.Bacc("TRN2", target_bir_lowering=False, num_devices=1)
    args = [nc.dram_tensor(k, v.shape, mybir.dt.from_np(v.dtype), kind="ExternalInput").ap() for k, v in arrays.items()]
    out = nc.dram_tensor("out", (4096, 128), F32, kind="ExternalOutput").ap()
    attention_and_product_keys(nc, *args, out)
    r = run_bass_kernel_spmd(nc, [arrays], core_ids=[0])
    return r.results[0]["out"].reshape(_OUT[0])
```

```python
from contextlib import ExitStack

import concourse.bass as bass
from concourse import mybir

ALU = mybir.AluOpType
ACT = mybir.ActivationFunctionType
AX_X = mybir.AxisListType.X
F32 = mybir.dt.float32
BF16 = mybir.dt.bfloat16
F16 = mybir.dt.float16

P = 128
HEADS = 16
DH = 8
W = 32
WIN = 3 * W
GROUPS = 4
BLOCKS = P // W
VW = 33
FF = 512
FC = FF // P
PK_HEADS = 8
KEYS = 32
TOPK = 8
EXPERTS = KEYS * KEYS
EC = EXPERTS // P
PH = 2 * PK_HEADS
EPS = 1e-5
MASKED = -1e30
FAR = -200.0
SLACK = 2.0 ** -21
TABLES = "natural_log_exp_and_others"


def attention_and_product_keys(nc, x, x_wrapped, ln1_g, ln1_b, ln2_g, ln2_b, w1, b1, w2, b2, w_q, w_qT,
                               gamma, beta, keysT, downT, up, out):
    tokens = x.shape[0]
    NT = tokens // P
    NQ = NT // 4
    TB = 8
    PAIRS = NT // 2

    with ExitStack() as ctx:
        def sb(name, shape, dt=F32):
            return ctx.enter_context(nc.sbuf_tensor(name, shape, dt))

        def sem(name):
            return ctx.enter_context(nc.semaphore(name))

        def two(name, shape, dt=F32):
            return [sb(f"{name}{p}", shape, dt) for p in range(2)]

        def two_sems(name):
            return [sem(f"{name}{p}") for p in range(2)]

        ps = ctx.enter_context(nc.psum_tensor("ps", [P, 8, 512], F32))

        ident = sb("ident", [P, P])
        ident_bf = sb("ident_bf", [P, P], BF16)
        ident_h = sb("ident_h", [P, P], F16)
        ones = sb("ones", [P, P])
        zeros = sb("zeros", [P, P + 1], BF16)
        minus_half = sb("minus_half", [P, 16])
        fold4 = sb("fold4", [P, W])
        spread4 = sb("spread4", [W, P])
        quadrant = sb("quadrant", [P, 4])
        head16 = sb("head16", [P, HEADS])
        head_in_group = sb("head_in_group", [P, 4])
        band = sb("band", [W, WIN])
        mask = sb("mask", [P, TB * BLOCKS * WIN], BF16)
        spread_keys = sb("spread_keys", [P, EXPERTS], F16)
        ln1_g_all = sb("ln1_g_all", [P, P])
        ln1_b_all = sb("ln1_b_all", [P, P])
        ln2_g_all = sb("ln2_g_all", [P, P])
        ln2_b_all = sb("ln2_b_all", [P, P])
        b2_all = sb("b2_all", [P, P])
        b1_col = sb("b1_col", [P, FC])
        w1_sb = sb("w1_sb", [P, FF])
        w2_sb = sb("w2_sb", [P, FC, P])
        wq_sb = sb("wq_sb", [P, PH * P])
        wqT_sb = sb("wqT_sb", [P, PH, P])
        keysT_sb = sb("keysT_sb", [P, PH, KEYS])
        gamma_sb = sb("gamma_sb", [P, PH])
        beta_sb = sb("beta_sb", [P, PH])
        downT_sb = sb("downT_sb", [P, EXPERTS])
        up_sb = sb("up_sb", [P, EC, P])

        xT = sb("xT", [P, W + tokens + W])
        kept = sb("kept", [P, tokens])

        x4 = two("x4", [P, 4, P])
        own_x = two("own_x", [P, P])
        windows = two("windows", [P, GROUPS, P + 2 * W])
        queries = two("queries", [P, BLOCKS, 4, W])
        v_raw = two("v_raw", [WIN, BLOCKS, P])
        v_ones = two("v_ones", [WIN, BLOCKS, GROUPS, VW])
        x_tile = two("x_tile", [P, P])
        row_max = two("row_max", [P, GROUPS * BLOCKS])
        SCORES = GROUPS * BLOCKS * WIN
        arena = sb("arena", [P, 4 * SCORES])
        shifted, probs = ([arena[:, (2 * a + p) * SCORES:(2 * a + p + 1) * SCORES].rearrange("p (k c) -> p k c", c=WIN)
                           for p in range(2)] for a in range(2))
        probsT = [sb(f"probsT{g}", [WIN, BLOCKS, P]) for g in range(GROUPS)]
        rdenom = two("rdenom", [P, 8])
        rdenom_own = two("rdenom_own", [P, 8, 4])
        heads_out = two("heads_out", [P, GROUPS * BLOCKS, W])
        r1_x1 = sb("r1_x1", [P, 4, 4, P])
        r1 = [r1_x1[:, q] for q in range(2)]
        x1 = [r1_x1[:, 2 + q] for q in range(2)]
        x1_b2 = two("x1_b2", [P, 4, P])
        x_lnb = two("x_lnb", [P, 4, P])
        x1T = sb("x1T", [P, 4 * P])
        hidT = sb("hidT", [P, FC, 4 * P])
        r2 = sb("r2", [P, 4, P])
        y2 = sb("y2", [P, 4, P])
        x3 = two("x3", [P, 4, P + 1])
        stats = sb("stats", [P, 12, 6])
        moments = sb("moments", [P, 12, 2])
        var_eps = sb("var_eps", [P, 12])
        rstd = sb("rstd", [P, 12])
        cov = sb("cov", [P, P + 1])
        mean_row = sb("mean_row", [1, P])
        prod = sb("prod", [P, PH, P])
        q_mean = sb("q_mean", [P, PH])
        q_var = sb("q_var", [P, PH])
        q_rstd = sb("q_rstd", [P, PH])
        q_scale = sb("q_scale", [P, PH])
        q_shift = sb("q_shift", [P, PH])
        keys_scaled = sb("keys_scaled", [P, PH, KEYS])
        keys_shifted = sb("keys_shifted", [P, PH, KEYS])
        w_sim = sb("w_sim", [P, PH * KEYS])
        c_sim = sb("c_sim", [P, PH * KEYS])
        xT_tile = two("xT_tile", [P, P])
        sim = two("sim", [P, PH, KEYS])
        top = two("top", [P, PH, TOPK])
        top_rel = sb("top_rel", [P, PH, TOPK])
        r3 = prod[:, 0:4, :]
        cand = prod[:, PK_HEADS:PK_HEADS + 4, :].rearrange("p a (b c d) -> p (a b) c d", b=2, c=TOPK)
        best = two("best", [P, PK_HEADS, TOPK])
        best_exp = two("best_exp", [P, PK_HEADS, TOPK])
        z = sb("z", [P, PK_HEADS])
        half_sums = sb("half_sums", [P, PK_HEADS, 4])
        quarter_sums = sb("quarter_sums", [P, PK_HEADS, 2])
        ln_z = sb("ln_z", [P, PK_HEADS])
        last_arg = sb("last_arg", [P, PK_HEADS])
        minus_lnz = two("minus_lnz", [P, PK_HEADS])
        threshold = two("threshold", [P, PK_HEADS])
        sim_rel = sb("sim_rel", [P, PH, KEYS])
        parts = sb("parts", [P, PK_HEADS, 4, KEYS], F16)
        partsT = two("partsT", [P, PK_HEADS, P], F16)
        expgrid = [arena[:, k * EXPERTS:(k + 1) * EXPERTS] for k in range(4)] \
            + [wq_sb[:, k * EXPERTS:(k + 1) * EXPERTS] for k in range(2)] \
            + [wqT_sb[:].rearrange("p a d -> p (a d)")[:, k * EXPERTS:(k + 1) * EXPERTS] for k in range(2)]
        weights = [arena[:, (4 + k) * EXPERTS:(5 + k) * EXPERTS] for k in range(2)] \
            + [r1_x1[:].rearrange("p a b c -> p (a b c)")[:, k * EXPERTS:(k + 1) * EXPERTS] for k in range(2)]
        RING = len(weights)
        act = [hidT[:, 2 * p:2 * p + 2, :].rearrange("p c i -> p (c i)") for p in range(2)]
        gated = prod[:, 0:EC, :]
        out_tile = two("out_tile", [P, P])
        res4 = sb("res4", [P, P])
        stats4 = sb("stats4", [P, 6])
        mom4 = sb("mom4", [P, 2])
        var4 = sb("var4", [P, 1])
        rstd4 = sb("rstd4", [P, 1])

        weights_in = sem("weights_in")
        ident_ready = sem("ident_ready")
        consts_ready = sem("consts_ready")
        band_ready = sem("band_ready")
        band_spread = sem("band_spread")
        mask_ready = sem("mask_ready")
        x4_in = two_sems("x4_in")
        a_transposed = sem("a_transposed")
        a_copied = sem("a_copied")
        v_in = two_sems("v_in")
        x_in = two_sems("x_in")
        operands_ready = sem("operands_ready")
        windows_ready = sem("windows_ready")
        v_ready = sem("v_ready")
        scores_done = sem("scores_done")
        max_done = sem("max_done")
        shift_done = sem("shift_done")
        exp_done = sem("exp_done")
        pt_done = sem("pt_done")
        pt_copied = sem("pt_copied")
        pv_done = sem("pv_done")
        norm_step = sem("norm_step")
        norm_done = sem("norm_done")
        attn_done = sem("attn_done")
        r1_done = sem("r1_done")
        seq = sem("seq")
        r1_staged = sem("r1_staged")
        xlnb_ready = sem("xlnb_ready")
        stat_step = sem("stat_step")
        var_done = sem("var_done")
        rstd_done = sem("rstd_done")
        ln_step = sem("ln_step")
        x1_done = sem("x1_done")
        x1b2_done = sem("x1b2_done")
        x1T_done = sem("x1T_done")
        x1T_copied = sem("x1T_copied")
        ff1_done = sem("ff1_done")
        relu_done = sem("relu_done")
        ff2_done = sem("ff2_done")
        r2_done = sem("r2_done")
        x3_done = sem("x3_done")
        x3_kept = sem("x3_kept")
        x3T_done = sem("x3T_done")
        x3T_copied = sem("x3T_copied")
        gram_done = sem("gram_done")
        r2_normed = sem("r2_normed")
        r2_scaled = sem("r2_scaled")
        r3_done = sem("r3_done")
        c_var = sem("c_var")
        c_pe = sem("c_pe")
        c_dve = sem("c_dve")
        c_pool = sem("c_pool")
        xT_staged = sem("xT_staged")
        down_done = sem("down_done")
        gelu_done = sem("gelu_done")
        sim_done = sem("sim_done")
        sim_copied = sem("sim_copied")
        top_done = sem("top_done")
        top_step = sem("top_step")
        cand_ready = sem("cand_ready")
        best_done = sem("best_done")
        bestexp_done = sem("bestexp_done")
        z_step = sem("z_step")
        z_done = sem("z_done")
        args_done = sem("args_done")
        lnz_done = sem("lnz_done")
        minus_lnz_done = sem("minus_lnz_done")
        threshold_done = sem("threshold_done")
        part_step = sem("part_step")
        parts_done = sem("parts_done")
        partsT_done = sem("partsT_done")
        partsT_copied = sem("partsT_copied")
        grid_done = sem("grid_done")
        gridexp_done = sem("gridexp_done")
        weighed = sem("weighed")
        summed = sem("summed")
        gated_done = sem("gated_done")
        up_done = sem("up_done")
        res_done = sem("res_done")
        d_step = sem("d_step")
        d_var = sem("d_var")
        d_rstd = sem("d_rstd")
        out_ready = sem("out_ready")
        stored = two_sems("stored")

        N_WEIGHTS = 15
        block = ctx.enter_context(nc.Block())

        def need(eng, s, n):
            if not isinstance(n, int) or n > 0:
                eng.wait_ge(s, n)

        def hold(eng):
            eng.sem_inc(seq, 1)

        def over_pairs(eng, n, body):
            body(0, True, False)
            with eng.Fori(1, n - 1) as i:
                body(i, False, False)
            body(n - 1, False, True)

        def bcast(ap, dim, n):
            wide = ap.unsqueeze(dim)
            return wide.broadcast_to([n if d == dim else size for d, size in enumerate(wide.shape)])

        def stretch(ap, n):
            return ap.broadcast_to(list(ap.shape[:-1]) + [n])

        def tok(t, n=P):
            return bass.ds(t * P, n)

        @block.sync
        def _(sp):
            for q in range(2):
                sp.dma_start(x4[q][:], x[q * 512:(q + 1) * 512, :].rearrange("(a p) d -> p a d", p=P)).then_inc(x4_in[q], 16)
            row = lambda v: v.rearrange("(a d) -> a d", a=1).broadcast_to([P, P])
            for dst, src in (
                (ln1_g_all[:], row(ln1_g)), (ln1_b_all[:], row(ln1_b)), (ln2_g_all[:], row(ln2_g)),
                (ln2_b_all[:], row(ln2_b)), (b2_all[:], row(b2)),
                (b1_col[:], b1), (w1_sb[:], w1), (w2_sb[:], w2.rearrange("(c p) d -> p c d", p=P)),
                (wq_sb[:], w_q), (wqT_sb[:], w_qT), (keysT_sb[:], keysT), (gamma_sb[:], gamma), (beta_sb[:], beta),
                (downT_sb[:], downT), (up_sb[:], up.rearrange("(c p) d -> p c d", p=P)),
            ):
                sp.dma_start(dst, src).then_inc(weights_in, 16)
            with sp.Fori(1, NQ // 2) as i:
                for q in range(2):
                    sp.wait_ge(a_transposed, 2 * i + q - 1)
                    sp.dma_start(x4[q][:], x[bass.ds((2 * i + q) * 512, 512), :].rearrange("(a p) d -> p a d", p=P)
                                 ).then_inc(x4_in[q], 16)

            def b1_loads(i, first, last):
                for p in range(2):
                    t = 2 * i + p
                    need(sp, v_ready, t - 1)
                    for b in range(BLOCKS):
                        sp.dma_start(v_raw[p][:, b, :], x_wrapped[bass.ds(t * P + b * W, WIN), :]).then_inc(v_in[p], 16)
                    need(sp, r1_done, t - 1)
                    sp.dma_start(x_tile[p][:], x[tok(t), :]).then_inc(x_in[p], 16)
            over_pairs(sp, PAIRS, b1_loads)

            def b2_loads(i, first, last):
                for q in range(2):
                    n = 2 * i + q
                    if first:
                        sp.wait_ge(a_transposed, NQ)
                    need(sp, xlnb_ready, n - 1)
                    sp.dma_start(x4[q][:], x[bass.ds(n * 512, 512), :].rearrange("(a p) d -> p a d", p=P)
                                 ).then_inc(x4_in[q], 16)
            over_pairs(sp, NQ // 2, b2_loads)

            def stores(i, first, last):
                for p in range(2):
                    t = 2 * i + p
                    sp.wait_ge(out_ready, t + 1)
                    sp.dma_start(out[tok(t), :], out_tile[p][:]).then_inc(stored[p], 16)
            over_pairs(sp, PAIRS, stores)
            for p in range(2):
                sp.wait_ge(stored[p], 16 * PAIRS + 16)

        @block.gpsimd
        def _(pool):
            nc.gpsimd.memset(minus_half[:], -0.5)
            nc.gpsimd.memset(ones[:], 1.0)
            nc.gpsimd.memset(zeros[:], 0.0)
            nc.gpsimd.memset(xT[:, 0:W], 0.0)
            nc.gpsimd.memset(xT[:, W + tokens:W + tokens + W], 0.0)
            for q in range(2):
                nc.gpsimd.memset(v_ones[q][:], 1.0)
                nc.gpsimd.memset(x3[q][:], 1.0)
            nc.gpsimd.memset(band[:], 0.0)
            nc.gpsimd.memset(ident[:], 0.0).then_inc(ident_ready, 1)
            pool.wait_ge(ident_ready, 1)
            nc.gpsimd.affine_select(out=ident[:], in_=ident[:], compare_op=ALU.not_equal, fill=1.0, base=0,
                                    pattern=[[-1, P]], channel_multiplier=1).then_inc(ident_ready, 1)
            nc.gpsimd.affine_select(out=band[:], in_=band[:], compare_op=ALU.is_ge, fill=MASKED, base=0,
                                    pattern=[[1, WIN]], channel_multiplier=-1).then_inc(band_ready, 1)
            pool.wait_ge(band_ready, 1)
            nc.gpsimd.affine_select(out=band[:], in_=band[:], compare_op=ALU.is_ge, fill=MASKED, base=2 * W,
                                    pattern=[[-1, WIN]], channel_multiplier=1).then_inc(band_ready, 1)
            pool.wait_ge(consts_ready, 6)
            pool.wait_ge(a_copied, NQ)

            def b1_operands(i, first, last):
                for p in range(2):
                    t = 2 * i + p
                    need(pool, scores_done, GROUPS * (t - 1))
                    hold(pool)
                    nc.gpsimd.tensor_copy(own_x[p][:], xT[:, bass.ds(t * P + W, P)]).then_inc(operands_ready, 1)
                    pool.wait_ge(operands_ready, 5 * t + 1)
                    hold(pool)
                    own = own_x[p][:].rearrange("p (b j) -> p b j", b=BLOCKS)
                    for h in range(4):
                        nc.gpsimd.tensor_scalar(queries[p][:, :, h, :], own, head_in_group[:, h:h + 1], None,
                                                ALU.mult).then_inc(operands_ready, 1)
                    need(pool, v_in[p], 16 * BLOCKS * (i + 1))
                    need(pool, pv_done, GROUPS * (t - 1))
                    hold(pool)
                    nc.gpsimd.tensor_copy(v_ones[p][:, :, :, 0:32].rearrange("p b g d -> p (b g) d"),
                                          v_raw[p][:].rearrange("p b (g d) -> p (b g) d", g=GROUPS)).then_inc(v_ready, 1)
            over_pairs(pool, PAIRS, b1_operands)

            pool.wait_ge(weights_in, 16 * N_WEIGHTS)

            def rsqrt(k, lo, hi):
                pool.wait_ge(var_done, k + 1)
                hold(pool)
                nc.gpsimd.tensor_tensor(rstd[:, 4 * lo:4 * hi], var_eps[:, 4 * lo:4 * hi], minus_half[:, 4 * lo:4 * hi],
                                        ALU.pow).then_inc(rstd_done, 1)

            def x_and_bias(n, i, q):
                pool.wait_ge(x4_in[q], 16 * (NQ // 2) + 16 * (i + 1))
                need(pool, r3_done, n - 1)
                hold(pool)
                nc.gpsimd.tensor_tensor(x_lnb[q][:], x4[q][:], bcast(ln2_b_all[:], 1, 4), ALU.add
                                        ).then_inc(xlnb_ready, 1)

            def x1_and_bias(n, q):
                pool.wait_ge(x1_done, n + 1)
                need(pool, r2_done, n - 1)
                hold(pool)
                nc.gpsimd.tensor_tensor(x1_b2[q][:], x1[q], bcast(b2_all[:], 1, 4), ALU.add
                                        ).then_inc(x1b2_done, 1)

            rsqrt(0, 1, 2)
            x_and_bias(0, 0, 0)
            rsqrt(1, 1, 2)
            x1_and_bias(0, 0)

            def b2_pool(i, first, last):
                for q in range(2):
                    n = 2 * i + q
                    rsqrt(2 * n + 2, 2 if last else 1, 2 if first and q == 0 else 3)
                    rsqrt(2 * n + 3, 0, 1)
                    if not (last and q == 1):
                        x1_and_bias(n + 1, 1 - q)
                        x_and_bias(n + 1, i + q, 1 - q)
            over_pairs(pool, NQ // 2, b2_pool)
            rsqrt(2 * NQ + 2, 2, 3)

            pool.wait_ge(c_dve, 5)
            hold(pool)
            nc.gpsimd.tensor_tensor(q_rstd[:], q_var[:], minus_half[:, 0:PH], ALU.pow).then_inc(c_pool, 1)

            pool.wait_ge(x3T_copied, NQ)

            def stage_x(t, p):
                need(pool, sim_done, t - 1)
                hold(pool)
                nc.gpsimd.tensor_copy(xT_tile[p][:], xT[:, tok(t)]).then_inc(xT_staged, 1)

            def split(t, p):
                pool.wait_ge(top_done, t + 1)
                hold(pool)
                nc.gpsimd.tensor_tensor(sim_rel[:], sim[p][:], stretch(top[p][:, :, 0:1], KEYS), ALU.subtract
                                        ).then_inc(part_step, 1)
                pool.wait_ge(part_step, 3 * t + 1)
                hold(pool)
                nc.gpsimd.tensor_scalar(sim_rel[:], sim_rel[:], FAR, None, ALU.max).then_inc(part_step, 1)
                pool.wait_ge(part_step, 3 * t + 2)
                need(pool, partsT_done, t)
                hold(pool)
                view = parts[:].rearrange("p h (a b) k -> p a b h k", a=2)
                rel = sim_rel[:].rearrange("p (a h) k -> p a h k", a=2)
                nc.gpsimd.tensor_copy(view[:, :, 0], rel).then_inc(part_step, 1)
                pool.wait_ge(part_step, 3 * t + 3)
                hold(pool)
                nc.gpsimd.tensor_tensor(view[:, :, 1], rel, view[:, :, 0], ALU.subtract).then_inc(parts_done, 1)

            def candidates(t, p):
                nc.gpsimd.tensor_tensor(top_rel[:], top[p][:], stretch(top[p][:, :, 0:1], TOPK), ALU.subtract
                                        ).then_inc(top_step, 1)
                pool.wait_ge(top_step, t + 1)
                need(pool, best_done, t)
                hold(pool)
                nc.gpsimd.tensor_tensor(cand, bcast(top_rel[:, 0:PK_HEADS, :], 3, TOPK),
                                        bcast(top_rel[:, PK_HEADS:PH, :], 2, TOPK), ALU.add).then_inc(cand_ready, 1)

            def normaliser(t, p):
                pool.wait_ge(bestexp_done, t + 1)
                hold(pool)
                e = best_exp[p]
                nc.gpsimd.tensor_tensor(half_sums[:], e[:, :, 0:4], e[:, :, 4:8], ALU.add).then_inc(z_step, 1)
                pool.wait_ge(z_step, 2 * t + 1)
                hold(pool)
                nc.gpsimd.tensor_tensor(quarter_sums[:], half_sums[:, :, 0:2], half_sums[:, :, 2:4], ALU.add
                                        ).then_inc(z_step, 1)
                pool.wait_ge(z_step, 2 * t + 2)
                hold(pool)
                nc.gpsimd.tensor_tensor(z[:], quarter_sums[:, :, 0], quarter_sums[:, :, 1], ALU.add).then_inc(z_done, 1)
                pool.wait_ge(lnz_done, t + 1)
                need(pool, gridexp_done, PK_HEADS * (t - 1))
                hold(pool)
                nc.gpsimd.tensor_scalar(minus_lnz[p][:], ln_z[:], -1.0, None, ALU.mult).then_inc(minus_lnz_done, 1)
                nc.gpsimd.tensor_scalar(last_arg[:], best[p][:, :, TOPK - 1], 1.0 + SLACK, -SLACK, ALU.mult, ALU.add
                                        ).then_inc(minus_lnz_done, 1)
                pool.wait_ge(minus_lnz_done, 2 * t + 2)
                hold(pool)
                nc.gpsimd.tensor_tensor(last_arg[:], last_arg[:], minus_lnz[p][:], ALU.add).then_inc(args_done, 1)

            stage_x(0, 0)
            stage_x(1, 1)
            split(0, 0)
            candidates(0, 0)
            normaliser(0, 0)

            split(1, 1)
            candidates(1, 1)

            def d_pool(i, first, last):
                for p in range(2):
                    t = 2 * i + p
                    if not last:
                        stage_x(t + 2, p)
                    if not (first and p == 0):
                        pool.wait_ge(d_var, t)
                        hold(pool)
                        nc.gpsimd.tensor_tensor(rstd4[:], var4[:], minus_half[:, 0:1], ALU.pow).then_inc(d_rstd, 1)
                    if not (last and p == 1):
                        normaliser(t + 1, 1 - p)
                    if not last:
                        split(t + 2, p)
                        candidates(t + 2, p)
            over_pairs(pool, PAIRS, d_pool)
            pool.wait_ge(d_var, NT)
            hold(pool)
            nc.gpsimd.tensor_tensor(rstd4[:], var4[:], minus_half[:, 0:1], ALU.pow).then_inc(d_rstd, 1)

        @block.tensor
        def _(pe):
            pe.wait_ge(ident_ready, 2)

            def a_transpose(i, first, last):
                for q in range(2):
                    n = 2 * i + q
                    pe.wait_ge(x4_in[q], 16 * (i + 1))
                    need(pe, a_copied, n - 1)
                    for a in range(4):
                        mm = nc.tensor.transpose(ps[:, q, a * P:(a + 1) * P], x4[q][:, a, :], ident[:])
                    mm.then_inc(a_transposed, 1)
            over_pairs(pe, NQ // 2, a_transpose)

            pe.wait_ge(consts_ready, 6)
            pe.wait_ge(band_ready, 2)
            nc.tensor.matmul(ps[:, 2, 0:WIN], spread4[:], band[:], start=True, stop=True).then_inc(band_spread, 1)
            pe.wait_ge(mask_ready, 3)

            def scores(t, p, half, mask_at):
                groups = (2 * half, 2 * half + 1)
                if half == 0:
                    pe.wait_ge(operands_ready, 5 * (t + 1))
                    pe.wait_ge(windows_ready, t + 1)
                    if isinstance(t, int) and t == 0:
                        pe.wait_ge(a_copied, NQ)
                need(pe, shift_done, 2 * (t - 1) + half + 1)
                for g in groups:
                    nc.tensor.matmul(ps[:, g, 0:BLOCKS * WIN], ident_bf[:], mask[:, mask_at], start=True, stop=False,
                                     skip_group_check=True)
                for b in range(BLOCKS):
                    for g in groups:
                        mm = nc.tensor.matmul(ps[:, g, b * WIN:(b + 1) * WIN], queries[p][:, b],
                                              windows[p][:, g, b * W:b * W + WIN], start=False, stop=True,
                                              skip_group_check=True)
                        if b == BLOCKS - 1:
                            mm.then_inc(scores_done, 1)

            def probs_transpose(t, p, half):
                pe.wait_ge(exp_done, 2 * t + half + 1)
                if half == 0:
                    need(pe, r1_done, t - 1)
                for g in (2 * half, 2 * half + 1):
                    need(pe, pt_copied, GROUPS * t + g - 1)
                    for b in range(BLOCKS):
                        mm = nc.tensor.transpose(ps[0:WIN, 4 + g % 2, b * P:(b + 1) * P],
                                                 probs[p][:, g * BLOCKS + b, :], ident[:])
                    mm.then_inc(pt_done, 1)

            def values(t, p, half):
                if half == 0:
                    pe.wait_ge(v_ready, t + 1)
                need(pe, norm_done, 2 * (t - 1) + half + 1)
                for g in (2 * half, 2 * half + 1):
                    pe.wait_ge(pt_copied, GROUPS * t + g + 1)
                    for b in range(BLOCKS):
                        k = (g % 2) * BLOCKS + b
                        mm = nc.tensor.matmul(ps[:, 6 + half, k * VW:(k + 1) * VW], probsT[g][:, b, :],
                                              v_ones[p][:, b, g, :], start=True, stop=True)
                    mm.then_inc(pv_done, 1)

            def attn_out(t, p, copied):
                pe.wait_ge(norm_done, 2 * t + 2)
                pe.wait_ge(pt_copied, copied)
                view = heads_out[p][:].rearrange("p (g b) c -> p b g c", g=GROUPS)
                for b in range(BLOCKS):
                    mm = nc.tensor.matmul(ps[32 * b:32 * b + 32, 4, 0:P], fold4[:], view[:, b], start=True, stop=True)
                mm.then_inc(attn_done, 1)

            def mask_of(r):
                return bass.ds(r * BLOCKS * WIN, BLOCKS * WIN)

            def b1_tile(t, p, r_next, first, last):
                more = not (last and p == 1)
                probs_transpose(t, p, 0)
                if more:
                    scores(t + 1, 1 - p, 0, mask_of(r_next))
                probs_transpose(t, p, 1)
                values(t, p, 0)
                if not (first and p == 0):
                    attn_out(t - 1, 1 - p, GROUPS * t + 3)
                if more:
                    scores(t + 1, 1 - p, 1, mask_of(r_next))
                values(t, p, 1)

            for half in range(2):
                scores(0, 0, half, mask_of(0))
            BP = TB // 2
            for p in range(2):
                b1_tile(p, p, p + 1, True, False)
            with pe.Fori(1, BP) as j:
                b1_tile(2 * j, 0, 2 * j + 1, False, False)
                b1_tile(2 * j + 1, 1, (2 * j + 2) % TB, False, False)
            with pe.Fori(1, NT // TB - 1) as s:
                with pe.Fori(0, BP) as j:
                    b1_tile(s * TB + 2 * j, 0, 2 * j + 1, False, False)
                    b1_tile(s * TB + 2 * j + 1, 1, (2 * j + 2) % TB, False, False)
            with pe.Fori(0, BP - 1) as j:
                b1_tile(NT - TB + 2 * j, 0, 2 * j + 1, False, False)
                b1_tile(NT - TB + 2 * j + 1, 1, 2 * j + 2, False, False)
            for p in range(2):
                b1_tile(NT - 2 + p, p, TB - 1, False, True)
            attn_out(NT - 1, 1, GROUPS * NT)

            pe.wait_ge(weights_in, 16 * N_WEIGHTS)
            pe.wait_ge(shift_done, 2 * NT)
            pe.wait_ge(r1_done, NT)
            pe.wait_ge(norm_done, 2 * NT)
            nc.tensor.matmul(ps[:, 5, 0:P + 1], ident_bf[:], zeros[:], start=True, stop=False,
                             skip_group_check=True)

            def feed_forward(n, q):
                pe.wait_ge(x1_done, n + 1)
                need(pe, x1T_copied, n)
                for a in range(4):
                    mm = nc.tensor.transpose(ps[:, 0, a * P:(a + 1) * P], x1[q][:, a, :], ident[:])
                mm.then_inc(x1T_done, 1)
                pe.wait_ge(x1T_copied, n + 1)
                for c in range(FC):
                    need(pe, relu_done, FC * n + c - 1)
                    nc.tensor.matmul(ps[:, 1 + c % 2, :], w1_sb[:, c * P:(c + 1) * P], x1T[:], start=True, stop=True
                                     ).then_inc(ff1_done, 1)
                pe.wait_ge(relu_done, FC * (n + 1))
                need(pe, r2_done, n)
                for a in range(4):
                    for c in range(FC):
                        mm = nc.tensor.matmul(ps[:, 3, a * P:(a + 1) * P], hidT[:, c, a * P:(a + 1) * P],
                                              w2_sb[:, c, :], start=(c == 0), stop=(c == FC - 1))
                mm.then_inc(ff2_done, 1)

            def result_products(n, q):
                pe.wait_ge(x3_done, n + 1)
                need(pe, x3T_copied, n)
                for a in range(4):
                    mm = nc.tensor.transpose(ps[:, 4, a * P:(a + 1) * P], x3[q][:, a, 0:P], ident[:])
                mm.then_inc(x3T_done, 1)
                for a in range(4):
                    mm = nc.tensor.matmul(ps[:, 5, 0:P + 1], x3[q][:, a, 0:P], x3[q][:, a, :], start=False, stop=True,
                                          skip_group_check=True)
                mm.then_inc(gram_done, 1)

            feed_forward(0, 0)

            def b2_pe(i, first, last):
                for q in range(2):
                    if not (last and q == 1):
                        feed_forward(2 * i + q + 1, 1 - q)
                    if not (first and q == 0):
                        result_products(2 * i + q - 1, 1 - q)
            over_pairs(pe, NQ // 2, b2_pe)
            result_products(NQ - 1, 1)

            pe.wait_ge(c_dve, 1)
            nc.tensor.matmul(ps[0:1, 6, 0:P], cov[:, P:P + 1], ident[:], start=True, stop=True).then_inc(c_pe, 1)
            pe.wait_ge(c_dve, 2)
            nc.tensor.matmul(ps[:, 7, 0:P], mean_row[:], mean_row[:], start=True, stop=True).then_inc(c_pe, 1)
            pe.wait_ge(c_dve, 3)
            pe.wait_ge(x3T_copied, NQ)
            for k in range(PH):
                mm = nc.tensor.matmul(ps[:, k // 3, (k % 3) * (P + 1):(k % 3 + 1) * (P + 1)],
                                      wq_sb[:, k * P:(k + 1) * P], cov[:], start=True, stop=True)
            mm.then_inc(c_pe, 1)
            pe.wait_ge(c_dve, 8)
            for k in range(PH):
                nc.tensor.matmul(ps[:, 6, k * KEYS:(k + 1) * KEYS], wqT_sb[:, k, :], keys_scaled[:, k, :],
                                 start=True, stop=True)
            nc.tensor.matmul(ps[:, 7, :], ones[:], keys_shifted[:].rearrange("p a k -> p (a k)"), start=True, stop=True
                             ).then_inc(c_pe, 1)
            pe.wait_ge(c_dve, 10)

            def down(t, p, sims=0):
                for half in range(2):
                    if p == 1:
                        pe.wait_ge(gelu_done, 2 * t + half - 1)
                    elif half == 0:
                        need(pe, res_done, t)
                    else:
                        pe.wait_ge(partsT_copied, t + 2)
                        pe.wait_ge(sim_copied, sims)
                    for c in range(4 * half, 4 * half + 4):
                        mm = nc.tensor.matmul(ps[:, 6 + half, (c % 4) * P:(c % 4 + 1) * P],
                                              downT_sb[:, c * P:(c + 1) * P], xT[:, tok(t)], start=True, stop=True)
                    mm.then_inc(down_done, 1)

            def similarities(t, p):
                pe.wait_ge(xT_staged, t + 1)
                need(pe, partsT_copied, t)
                nc.tensor.matmul(ps[:, 7, :], xT_tile[p][:], w_sim[:], start=True, stop=True).then_inc(sim_done, 1)

            def parts_transpose(t, p):
                pe.wait_ge(parts_done, t + 1)
                pe.wait_ge(sim_copied, t + 1)
                if p == 0:
                    need(pe, gelu_done, 2 * t)
                bank = ps[:, 7, :].bitcast(F16)
                for h in range(PK_HEADS):
                    mm = nc.tensor.transpose(bank[:, h * P:(h + 1) * P], parts[:, h].rearrange("p a k -> p (a k)"),
                                             ident_h[:])
                mm.then_inc(partsT_done, 1)

            def grid(t, p, h):
                if h == 0:
                    pe.wait_ge(partsT_copied, t + 1)
                need(pe, gridexp_done, PK_HEADS * t + h - 1)
                for half in range(2):
                    mm = nc.tensor.matmul(ps[:, 2 * (h % 2) + half, :], partsT[p][:, h, :],
                                          spread_keys[:, half * 512:(half + 1) * 512], start=True, stop=True)
                mm.then_inc(grid_done, 1)

            def sum_heads(t, h):
                pe.wait_ge(weighed, PK_HEADS * t + h + 1)
                if h == 0:
                    need(pe, gated_done, t)
                for c in range(EC):
                    mm = nc.tensor.matmul(ps[:, 4 + c // 4, (c % 4) * P:(c % 4 + 1) * P],
                                          weights[h % RING][:, c * P:(c + 1) * P], ident[:], is_transpose=True,
                                          start=(h == 0 and c % 4 == 0), stop=(h == PK_HEADS - 1),
                                          skip_group_check=True)
                mm.then_inc(summed, 1)

            def up_projection(t, gelus):
                pe.wait_ge(gated_done, t + 1)
                pe.wait_ge(gelu_done, gelus)
                for c in range(EC):
                    mm = nc.tensor.matmul(ps[:, 6, 0:P], gated[:, c, :], up_sb[:, c, :], start=(c == 0),
                                          stop=(c == EC - 1))
                mm.then_inc(up_done, 1)

            similarities(0, 0)
            parts_transpose(0, 0)
            similarities(1, 1)
            grid(0, 0, 0)
            grid(0, 0, 1)

            def d_pe(i, first, last):
                for p in range(2):
                    t = 2 * i + p
                    more = not (last and p == 1)
                    grid(t, p, 2)
                    grid(t, p, 3)
                    if more:
                        parts_transpose(t + 1, 1 - p)
                    if not (first and p == 0):
                        up_projection(t - 1, 4 * (i + p))
                    grid(t, p, 4)
                    sum_heads(t, 0)
                    grid(t, p, 5)
                    sum_heads(t, 1)
                    grid(t, p, 6)
                    if not last:
                        similarities(t + 2, p)
                    sum_heads(t, 2)
                    grid(t, p, 7)
                    sum_heads(t, 3)
                    if more:
                        grid(t + 1, 1 - p, 0)
                    if p == 0:
                        down(t, 0, NT if last else t + 3)
                    sum_heads(t, 4)
                    if p == 0:
                        down(t + 1, 1)
                    sum_heads(t, 5)
                    if more:
                        grid(t + 1, 1 - p, 1)
                    sum_heads(t, 6)
                    sum_heads(t, 7)
            over_pairs(pe, PAIRS, d_pe)
            up_projection(NT - 1, 2 * NT)

        @block.scalar
        def _(a):
            def copy(out_ap, in_ap):
                return nc.scalar.activation(out_ap, in_ap, ACT.Copy)

            def a_copy(i, first, last):
                for q in range(2):
                    n = 2 * i + q
                    a.wait_ge(a_transposed, n + 1)
                    copy(xT[:, bass.ds(W + n * 512, 512)], ps[:, q, :]).then_inc(a_copied, 1)
            over_pairs(a, NQ // 2, a_copy)

            def exps(t, p):
                for half in range(2):
                    a.wait_ge(shift_done, 2 * t + half + 1)
                    need(a, pt_done, GROUPS * (t - 2) + 2 * half + 2)
                    s = slice(8 * half, 8 * half + 8)
                    nc.scalar.activation(probs[p][:, s, :], shifted[p][:, s, :], ACT.Exp).then_inc(exp_done, 1)

            def probs_copy(t):
                for g in range(GROUPS):
                    a.wait_ge(pt_done, GROUPS * t + g + 1)
                    need(a, pv_done, GROUPS * (t - 1) + g + 1)
                    copy(probsT[g][:].rearrange("p b i -> p (b i)"), ps[0:WIN, 4 + g % 2, :]).then_inc(pt_copied, 1)

            exps(0, 0)

            def b1_act(i, first, last):
                for p in range(2):
                    probs_copy(2 * i + p)
                    if not (last and p == 1):
                        exps(2 * i + p + 1, 1 - p)
            over_pairs(a, PAIRS, b1_act)

            a.wait_ge(weights_in, 16 * N_WEIGHTS)

            def hidden(n):
                a.wait_ge(x1T_done, n + 1)
                need(a, ff1_done, FC * n)
                copy(x1T[:], ps[:, 0, :]).then_inc(x1T_copied, 1)
                need(a, ff2_done, n)
                for c in range(FC):
                    a.wait_ge(ff1_done, FC * n + c + 1)
                    nc.scalar.activation(hidT[:, c, :], ps[:, 1 + c % 2, :], ACT.Relu, bias=b1_col[:, c:c + 1]
                                         ).then_inc(relu_done, 1)

            def stage(n, q):
                a.wait_ge(r1_done, 4 * n + 4)
                need(a, x1_done, n - 1)
                copy(r1[q].rearrange("p a d -> p (a d)"), kept[:, bass.ds(n * 512, 512)]).then_inc(r1_staged, 1)

            def results(n, q):
                a.wait_ge(x3_done, n + 1)
                copy(kept[:, bass.ds(n * 512, 512)].rearrange("p (a d) -> p a d", a=4), x3[q][:, :, 0:P]
                     ).then_inc(x3_kept, 1)
                a.wait_ge(x3T_done, n + 1)
                copy(xT[:, bass.ds(n * 512, 512)], ps[:, 4, :]).then_inc(x3T_copied, 1)

            stage(0, 0)
            stage(1, 1)
            hidden(0)

            def b2_act(i, first, last):
                for q in range(2):
                    n = 2 * i + q
                    if not last:
                        stage(n + 2, q)
                    if not (last and q == 1):
                        hidden(n + 1)
                    if not (first and q == 0):
                        results(n - 1, 1 - q)
            over_pairs(a, NQ // 2, b2_act)
            results(NQ - 1, 1)

            def gelus(t, p):
                need(a, gated_done, t - 1)
                for half in range(2):
                    a.wait_ge(down_done, 2 * t + half + 1)
                    nc.scalar.activation(act[p][:, half * 512:(half + 1) * 512], ps[:, 6 + half, :],
                                         ACT.Gelu_apprx_tanh).then_inc(gelu_done, 1)

            def best_exps(t, p):
                a.wait_ge(best_done, t + 1)
                nc.scalar.activation(best_exp[p][:], best[p][:], ACT.Exp).then_inc(bestexp_done, 1)

            def log_z(t):
                a.wait_ge(z_done, t + 1)
                nc.scalar.activation(ln_z[:], z[:], ACT.Ln).then_inc(lnz_done, 1)

            def thresholds(t, p):
                a.wait_ge(args_done, t + 1)
                need(a, weighed, PK_HEADS * (t - 1))
                nc.scalar.activation(threshold[p][:], last_arg[:], ACT.Exp).then_inc(threshold_done, 1)

            def parts_copy(t, p):
                a.wait_ge(partsT_done, t + 1)
                copy(partsT[p][:].rearrange("p h i -> p (h i)"), ps[:, 7, :].bitcast(F16)).then_inc(partsT_copied, 1)

            def grid_exp(t, p, h):
                a.wait_ge(grid_done, PK_HEADS * t + h + 1)
                need(a, weighed, PK_HEADS * (t - 1) + h + 1)
                nc.scalar.activation(expgrid[h], ps[:, 2 * (h % 2):2 * (h % 2) + 2, :].rearrange("p a b -> p (a b)"),
                                     ACT.Exp, bias=minus_lnz[p][:, h:h + 1]).then_inc(gridexp_done, 1)

            a.preload_act_table_set(TABLES)
            best_exps(0, 0)
            log_z(0)
            thresholds(0, 0)
            parts_copy(0, 0)

            grid_exp(0, 0, 0)
            grid_exp(0, 0, 1)

            def d_act(i, first, last):
                for p in range(2):
                    t = 2 * i + p
                    more = not (last and p == 1)
                    grid_exp(t, p, 2)
                    grid_exp(t, p, 3)
                    grid_exp(t, p, 4)
                    if more:
                        parts_copy(t + 1, 1 - p)
                    grid_exp(t, p, 5)
                    if more:
                        best_exps(t + 1, 1 - p)
                    grid_exp(t, p, 6)
                    if more:
                        log_z(t + 1)
                    grid_exp(t, p, 7)
                    if more:
                        thresholds(t + 1, 1 - p)
                    if more:
                        grid_exp(t + 1, 1 - p, 0)
                    if p == 0:
                        gelus(t, 0)
                        gelus(t + 1, 1)
                        a.preload_act_table_set(TABLES)
                    if more:
                        grid_exp(t + 1, 1 - p, 1)
            over_pairs(a, PAIRS, d_act)

        @block.vector
        def _(v):
            V = nc.vector
            for p in range(2):
                v.sem_inc(stored[p], 16)
            v.wait_ge(ident_ready, 2)
            V.tensor_reduce(fold4[:], ident[:].rearrange("p (q c) -> p c q", q=4), AX_X, ALU.add).then_inc(consts_ready, 1)
            V.tensor_reduce(quadrant[:], ident[:].rearrange("p (q c) -> p q c", q=4), AX_X, ALU.add
                            ).then_inc(consts_ready, 1)
            V.tensor_reduce(head16[:], ident[:].rearrange("p (h e) -> p h e", e=DH), AX_X, ALU.add
                            ).then_inc(consts_ready, 1)
            V.tensor_copy(spread4[:].rearrange("p (q c) -> p q c", q=4), bcast(ident[0:W, 0:W], 1, 4)
                          ).then_inc(consts_ready, 1)
            V.tensor_copy(ident_bf[:], ident[:]).then_inc(consts_ready, 1)
            v.wait_ge(consts_ready, 5)
            V.tensor_reduce(head_in_group[:], head16[:].rearrange("p (q h) -> p h q", q=4), AX_X, ALU.add
                            ).then_inc(consts_ready, 1)
            V.tensor_copy(ident_h[:], ident[:])
            for q in range(4):
                rows = slice(32 * q, 32 * q + 32)
                one = ident[rows, 32 * q:32 * q + 32]
                V.tensor_copy(spread_keys[rows, :].rearrange("p (i j) -> p i j", i=KEYS),
                              bcast(one, 2, KEYS) if q < 2 else bcast(one, 1, KEYS))
            v.wait_ge(band_spread, 1)
            m = mask[:].rearrange("p (b c) -> p b c", c=WIN)
            V.tensor_copy(m, bcast(ps[:, 2, 0:WIN], 1, TB * BLOCKS)).then_inc(mask_ready, 1)
            v.wait_ge(mask_ready, 1)
            V.memset(m[:, 0, 0:W], MASKED).then_inc(mask_ready, 1)
            V.memset(m[:, TB * BLOCKS - 1, 2 * W:WIN], MASKED).then_inc(mask_ready, 1)

            def shift(t, p, half):
                at = 8 * half
                sc = ps[:, 2 * half:2 * half + 2, 0:BLOCKS * WIN].rearrange("p a (b c) -> p a b c", c=WIN)
                mx = row_max[p][:, at:at + 8]
                v.wait_ge(scores_done, GROUPS * t + 2 * half + 2)
                V.tensor_reduce(mx.rearrange("p (a b) -> p a b", a=2), sc, AX_X, ALU.max).then_inc(max_done, 1)
                v.wait_ge(max_done, 2 * t + half + 1)
                need(v, exp_done, 2 * (t - 2) + half + 1)
                V.tensor_tensor(shifted[p][:, at:at + 8, :].rearrange("p (a b) c -> p a b c", a=2), sc,
                                bcast(mx.rearrange("p (a b) -> p a b", a=2), 3, WIN), ALU.subtract
                                ).then_inc(shift_done, 1)

            def normalise(t, p, half):
                pv = ps[:, 6 + half, 0:8 * VW].rearrange("p (k c) -> p k c", c=VW)
                n = 2 * t + half
                v.wait_ge(pv_done, GROUPS * t + 2 * half + 2)
                V.reciprocal(rdenom[half][:], pv[:, :, 32]).then_inc(norm_step, 1)
                v.wait_ge(norm_step, 2 * n + 1)
                V.tensor_tensor(rdenom_own[half][:], bcast(rdenom[half][:], 2, 4), bcast(quadrant[:], 1, 8), ALU.mult
                                ).then_inc(norm_step, 1)
                v.wait_ge(norm_step, 2 * n + 2)
                if half == 0:
                    need(v, attn_done, t - 1)
                V.tensor_tensor(heads_out[p][:, 8 * half:8 * half + 8, :].rearrange("p k (h d) -> p k h d", h=4),
                                pv[:, :, 0:32].rearrange("p k (h d) -> p k h d", h=4),
                                bcast(rdenom_own[half][:], 3, DH), ALU.mult).then_inc(norm_done, 1)

            def residual(t, i, p):
                v.wait_ge(attn_done, t + 1)
                v.wait_ge(x_in[p], 16 * (i + 1))
                V.tensor_tensor(kept[:, tok(t)], ps[:, 4, 0:P], x_tile[p][:], ALU.add).then_inc(r1_done, 1)

            def group_windows(t, p):
                need(v, scores_done, GROUPS * (t - 1))
                V.tensor_tensor(windows[p][:], bcast(xT[:, tok(t, P + 2 * W)], 1, GROUPS),
                                bcast(quadrant[:], 2, P + 2 * W), ALU.mult).then_inc(windows_ready, 1)

            v.wait_ge(a_copied, NQ)
            group_windows(0, 0)
            group_windows(1, 1)
            shift(0, 0, 0)
            shift(0, 0, 1)

            def b1_dve(i, first, last):
                for p in range(2):
                    t = 2 * i + p
                    if not (last and p == 1):
                        shift(t + 1, 1 - p, 0)
                    if not last:
                        group_windows(t + 2, p)
                    normalise(t, p, 0)
                    if not (first and p == 0):
                        residual(t - 1, i if p == 1 else i - 1, 1 - p)
                    if not (last and p == 1):
                        shift(t + 1, 1 - p, 1)
                    normalise(t, p, 1)
            over_pairs(v, PAIRS, b1_dve)
            residual(NT - 1, PAIRS - 1, 1)

            v.wait_ge(weights_in, 16 * N_WEIGHTS)

            def ln_stats(norm, src):
                for a in range(4):
                    last = V.bn_stats(stats[:, 4 * norm + a, :], src[:, a, :])
                return last

            def ln_moments(k, lo, hi):
                v.wait_ge(stat_step, 2 * k + 1)
                hold(v)
                for j in range(4 * lo, 4 * hi):
                    last = V.bn_aggr(moments[:, j, :], stats[:, j, :])
                last.then_inc(stat_step, 1)
                v.wait_ge(stat_step, 2 * k + 2)
                V.tensor_scalar(var_eps[:, 4 * lo:4 * hi], moments[:, 4 * lo:4 * hi, 1], EPS, None, ALU.add
                                ).then_inc(var_done, 1)

            def ln_apply(norm, src, dst, done):
                for a in range(4):
                    j = 4 * norm + a
                    last = V.tensor_scalar(dst[:, a, :], src[:, a, :], moments[:, j, 0:1], rstd[:, j:j + 1],
                                           ALU.subtract, ALU.mult)
                last.then_inc(done, 1)

            def ln1_stats(n, q):
                v.wait_ge(r1_staged, n + 1)
                return ln_stats(1, r1[q])

            def ln1_apply(n, q):
                ln_apply(1, r1[q], y2, ln_step)
                v.wait_ge(ln_step, 2 * n + 1)
                V.tensor_tensor(y2[:], y2[:], bcast(ln1_g_all[:], 1, 4), ALU.mult).then_inc(ln_step, 1)
                v.wait_ge(ln_step, 2 * n + 2)
                need(v, x1b2_done, n - 1)
                need(v, x1T_done, n - 1)
                V.tensor_tensor(x1[q], y2[:], bcast(ln1_b_all[:], 1, 4), ALU.add).then_inc(x1_done, 1)

            def ln2_stats(n, q):
                v.wait_ge(ff2_done, n + 1)
                v.wait_ge(x1b2_done, n + 1)
                V.tensor_tensor(r2[:], ps[:, 3, :].rearrange("p (a d) -> p a d", a=4), x1_b2[q][:], ALU.add
                                ).then_inc(r2_done, 1)
                v.wait_ge(r2_done, n + 1)
                return ln_stats(0, r2)

            def ln2_apply(n, q):
                ln_apply(0, r2, r2, r2_normed)
                v.wait_ge(r2_normed, n + 1)
                V.tensor_tensor(r2[:], r2[:], bcast(ln2_g_all[:], 1, 4), ALU.mult).then_inc(r2_scaled, 1)
                v.wait_ge(r2_scaled, n + 1)
                v.wait_ge(xlnb_ready, n + 1)
                V.tensor_tensor(r3, r2[:], x_lnb[q][:], ALU.add).then_inc(r3_done, 1)

            def ln3_stats(n):
                v.wait_ge(r3_done, n + 1)
                return ln_stats(2, r3)

            def ln3_apply(n, q):
                need(v, gram_done, n - 1)
                need(v, x3_kept, n - 1)
                ln_apply(2, r3, x3[q][:, :, 0:P], x3_done)

            for n in range(2):
                ln1_stats(n, n).then_inc(stat_step, 1)
                ln_moments(n, 1, 2)
                v.wait_ge(rstd_done, n + 1)
                ln1_apply(n, n)

            def b2_dve(i, first, last):
                for q in range(2):
                    n = 2 * i + q
                    with_ln3 = not (first and q == 0)
                    if with_ln3:
                        step = ln3_stats(n - 1)
                    if not last:
                        step = ln1_stats(n + 2, q)
                    step.then_inc(stat_step, 1)
                    ln_moments(2 * n + 2, 2 if last else 1, 3 if with_ln3 else 2)
                    ln2_stats(n, q).then_inc(stat_step, 1)
                    ln_moments(2 * n + 3, 0, 1)
                    v.wait_ge(rstd_done, 2 * n + 3)
                    if not last:
                        ln1_apply(n + 2, q)
                    if with_ln3:
                        ln3_apply(n - 1, 1 - q)
                    v.wait_ge(rstd_done, 2 * n + 4)
                    ln2_apply(n, q)
            over_pairs(v, NQ // 2, b2_dve)
            ln3_stats(NQ - 1).then_inc(stat_step, 1)
            ln_moments(2 * NQ + 2, 2, 3)
            v.wait_ge(rstd_done, 2 * NQ + 3)
            ln3_apply(NQ - 1, 1)

            v.wait_ge(gram_done, NQ)
            V.tensor_scalar(cov[:], ps[:, 5, 0:P + 1], 1.0 / tokens, None, ALU.mult).then_inc(c_dve, 1)
            v.wait_ge(c_pe, 1)
            V.tensor_copy(mean_row[:], ps[0:1, 6, 0:P]).then_inc(c_dve, 1)
            v.wait_ge(c_pe, 2)
            V.scalar_tensor_tensor(cov[:, 0:P], ps[:, 7, 0:P], -1.0, cov[:, 0:P], ALU.mult, ALU.add).then_inc(c_dve, 1)
            v.wait_ge(c_pe, 3)
            for b in range(6):
                n = min(3, PH - 3 * b)
                z3 = ps[:, b, 0:n * (P + 1)].rearrange("p (k c) -> p k c", c=P + 1)
                V.tensor_tensor(prod[:, 3 * b:3 * b + n, :], z3[:, :, 0:P], wqT_sb[:, 3 * b:3 * b + n, :], ALU.mult)
                last = V.tensor_copy(q_mean[:, 3 * b:3 * b + n], z3[:, :, P])
            last.then_inc(c_dve, 1)
            v.wait_ge(c_dve, 4)
            V.tensor_reduce(q_var[:], prod[:], AX_X, ALU.add).then_inc(c_var, 1)
            v.wait_ge(c_var, 1)
            V.tensor_scalar(q_var[:], q_var[:], EPS, None, ALU.add).then_inc(c_dve, 1)
            v.wait_ge(c_pool, 1)
            V.tensor_tensor(q_scale[:], q_rstd[:], gamma_sb[:], ALU.mult).then_inc(c_var, 1)
            v.wait_ge(c_var, 2)
            V.tensor_tensor(q_shift[:], q_mean[:], q_scale[:], ALU.mult).then_inc(c_var, 1)
            v.wait_ge(c_var, 3)
            V.tensor_tensor(q_shift[:], beta_sb[:], q_shift[:], ALU.subtract).then_inc(c_dve, 1)
            v.wait_ge(c_dve, 6)
            V.tensor_tensor(keys_scaled[:], keysT_sb[:], bcast(q_scale[:], 2, KEYS), ALU.mult).then_inc(c_dve, 1)
            V.tensor_tensor(keys_shifted[:], keysT_sb[:], bcast(q_shift[:], 2, KEYS), ALU.mult).then_inc(c_dve, 1)
            v.wait_ge(c_pe, 4)
            V.tensor_copy(w_sim[:], ps[:, 6, :]).then_inc(c_dve, 1)
            V.tensor_copy(c_sim[:], ps[:, 7, :]).then_inc(c_dve, 1)
            v.wait_ge(c_dve, 10)

            def top_keys(t, p):
                v.wait_ge(sim_done, t + 1)
                need(v, part_step, 3 * (t - 2) + 1)
                V.tensor_tensor(sim[p][:].rearrange("p a k -> p (a k)"), ps[:, 7, :], c_sim[:], ALU.add
                                ).then_inc(sim_copied, 1)
                v.wait_ge(sim_copied, t + 1)
                hold(v)
                for k in range(PH):
                    last = V.max(top[p][:, k, :], sim[p][:, k, :])
                last.then_inc(top_done, 1)

            def top_pairs(t, p):
                v.wait_ge(cand_ready, t + 1)
                hold(v)
                for h in range(PK_HEADS):
                    last = V.max(best[p][:, h, :], cand[:, h].rearrange("p a b -> p (a b)"))
                last.then_inc(best_done, 1)

            def weigh(t, p, h):
                v.wait_ge(gridexp_done, PK_HEADS * t + h + 1)
                need(v, summed, PK_HEADS * t + h + 1 - RING)
                if h == 0:
                    v.wait_ge(threshold_done, t + 1)
                V.scalar_tensor_tensor(weights[h % RING], expgrid[h], threshold[p][:, h:h + 1], expgrid[h],
                                       ALU.is_ge, ALU.mult).then_inc(weighed, 1)

            def gate(t, p):
                v.wait_ge(summed, PK_HEADS * (t + 1))
                v.wait_ge(gelu_done, 2 * t + 2)
                need(v, up_done, t)
                V.tensor_tensor(gated.rearrange("p c i -> p (c i)"), ps[:, 4:6, :].rearrange("p a b -> p (a b)"),
                                act[p], ALU.mult).then_inc(gated_done, 1)

            def last_moments(t):
                v.wait_ge(up_done, t + 1)
                V.tensor_tensor(res4[:], ps[:, 6, 0:P], kept[:, tok(t)], ALU.add).then_inc(res_done, 1)
                v.wait_ge(res_done, t + 1)
                V.bn_stats(stats4[:], res4[:]).then_inc(d_step, 1)
                v.wait_ge(d_step, 2 * t + 1)
                hold(v)
                V.bn_aggr(mom4[:], stats4[:]).then_inc(d_step, 1)
                v.wait_ge(d_step, 2 * t + 2)
                V.tensor_scalar(var4[:], mom4[:, 1:2], EPS, None, ALU.add).then_inc(d_var, 1)

            def last_norm(t, i, p):
                v.wait_ge(d_rstd, t + 1)
                v.wait_ge(stored[p], 16 * i + 16)
                V.tensor_scalar(out_tile[p][:], res4[:], mom4[:, 0:1], rstd4[:], ALU.subtract, ALU.mult
                                ).then_inc(out_ready, 1)

            v.wait_ge(x3_kept, NQ)
            top_keys(0, 0)
            top_pairs(0, 0)

            top_keys(1, 1)
            weigh(0, 0, 0)

            def d_dve(i, first, last):
                for p in range(2):
                    t = 2 * i + p
                    more = not (last and p == 1)
                    before = not (first and p == 0)
                    weigh(t, p, 1)
                    weigh(t, p, 2)
                    if before:
                        last_moments(t - 1)
                    if more:
                        top_pairs(t + 1, 1 - p)
                    weigh(t, p, 3)
                    weigh(t, p, 4)
                    if not last:
                        top_keys(t + 2, p)
                    weigh(t, p, 5)
                    if before:
                        last_norm(t - 1, i if p == 1 else i - 1, 1 - p)
                    weigh(t, p, 6)
                    weigh(t, p, 7)
                    if more:
                        weigh(t + 1, 1 - p, 0)
                    gate(t, p)
            over_pairs(v, PAIRS, d_dve)
            last_moments(NT - 1)
            last_norm(NT - 1, PAIRS - 1, 1)


_OUT = ((4, 1024, 128), "float32")


def kernel(**inputs):
    import numpy as np
    import concourse.bacc as bacc
    from concourse.bass_utils import run_bass_kernel_spmd

    a = {k: np.asarray(v) for k, v in inputs.items()}
    x = a["L0_attn_src"].reshape(4096, 128)
    arrays = {
        "x": x,
        "x_wrapped": np.concatenate([x[-W:], x, x[:W]]),
        "ln1_g": a["L0_attn_ln1_g"], "ln1_b": a["L0_attn_ln1_b"],
        "ln2_g": a["L0_attn_ln2_g"], "ln2_b": a["L0_attn_ln2_b"],
        "w1": a["L0_attn_W1"], "b1": a["L0_attn_b1"].reshape(FC, P).T,
        "w2": a["L0_attn_W2"], "b2": a["L0_attn_b2"],
        "w_q": a["L0_ffn_w_q"], "w_qT": a["L0_ffn_w_q"].reshape(P, PH, P).transpose(2, 1, 0),
        "gamma": a["L0_ffn_bn_gamma"].reshape(PH, P).T, "beta": a["L0_ffn_bn_beta"].reshape(PH, P).T,
        "keysT": a["L0_ffn_keys"].transpose(3, 2, 0, 1).reshape(P, PH, KEYS),
        "downT": a["L0_ffn_down_embed"].T, "up": a["L0_ffn_up_embed"],
    }
    arrays = {f"in_{k}": np.ascontiguousarray(v) for k, v in arrays.items()}
    nc = bacc.Bacc("TRN2", target_bir_lowering=False, num_devices=1)
    args = [nc.dram_tensor(k, v.shape, mybir.dt.from_np(v.dtype), kind="ExternalInput").ap() for k, v in arrays.items()]
    out = nc.dram_tensor("out", (4096, 128), F32, kind="ExternalOutput").ap()
    attention_and_product_keys(nc, *args, out)
    r = run_bass_kernel_spmd(nc, [arrays], core_ids=[0])
    return r.results[0]["out"].reshape(_OUT[0])
```

```python
from contextlib import ExitStack

import concourse.bass as bass
from concourse import mybir

ALU = mybir.AluOpType
ACT = mybir.ActivationFunctionType
AX_X = mybir.AxisListType.X
F32 = mybir.dt.float32
BF16 = mybir.dt.bfloat16
F16 = mybir.dt.float16

P = 128
HEADS = 16
DH = 8
W = 32
WIN = 3 * W
GROUPS = 4
BLOCKS = P // W
VW = 33
FF = 512
FC = FF // P
PK_HEADS = 8
KEYS = 32
TOPK = 8
EXPERTS = KEYS * KEYS
EC = EXPERTS // P
PH = 2 * PK_HEADS
EPS = 1e-5
QB = 3
Q_SPLIT = (slice(0, 3 * QB), slice(3 * QB, PH))
MASKED = -1e30
FAR = -200.0
SLACK = 2.0 ** -21
TABLES = "natural_log_exp_and_others"


def attention_and_product_keys(nc, x, x_wrapped, ln1_g, ln1_b, ln2_g, ln2_b, w1, b1, w2, b2, w_q, w_qT,
                               gamma, beta, keysT, downT, up, out):
    tokens = x.shape[0]
    NT = tokens // P
    NQ = NT // 4
    TB = 8
    PAIRS = NT // 2

    with ExitStack() as ctx:
        def sb(name, shape, dt=F32):
            return ctx.enter_context(nc.sbuf_tensor(name, shape, dt))

        def sem(name):
            return ctx.enter_context(nc.semaphore(name))

        def two(name, shape, dt=F32):
            return [sb(f"{name}{p}", shape, dt) for p in range(2)]

        def two_sems(name):
            return [sem(f"{name}{p}") for p in range(2)]

        ps = ctx.enter_context(nc.psum_tensor("ps", [P, 8, 512], F32))

        ident = sb("ident", [P, P])
        ident_bf = sb("ident_bf", [P, P], BF16)
        ident_h = sb("ident_h", [P, P], F16)
        ones = sb("ones", [P, P])
        zeros = sb("zeros", [P, P + 1], BF16)
        minus_half = sb("minus_half", [P, 16])
        fold4 = sb("fold4", [P, W])
        spread4 = sb("spread4", [W, P])
        quadrant = sb("quadrant", [P, 4])
        head16 = sb("head16", [P, HEADS])
        head_in_group = sb("head_in_group", [P, 4])
        band = sb("band", [W, WIN])
        mask = sb("mask", [P, TB * BLOCKS * WIN], BF16)
        spread_keys = sb("spread_keys", [P, EXPERTS], F16)
        ln1_g_all = sb("ln1_g_all", [P, P])
        ln1_b_all = sb("ln1_b_all", [P, P])
        ln2_g_all = sb("ln2_g_all", [P, P])
        ln2_b_all = sb("ln2_b_all", [P, P])
        b2_all = sb("b2_all", [P, P])
        b1_col = sb("b1_col", [P, FC])
        w1_sb = sb("w1_sb", [P, FF])
        w2_sb = sb("w2_sb", [P, FC, P])
        wq_sb = sb("wq_sb", [P, PH * P])
        wqT_sb = sb("wqT_sb", [P, PH, P])
        keysT_sb = sb("keysT_sb", [P, PH, KEYS])
        gamma_sb = sb("gamma_sb", [P, PH])
        beta_sb = sb("beta_sb", [P, PH])
        downT_sb = sb("downT_sb", [P, EXPERTS])
        up_sb = sb("up_sb", [P, EC, P])

        xT = sb("xT", [P, W + tokens + W])
        kept = sb("kept", [P, tokens])

        own_x = two("own_x", [P, P])
        windows = two("windows", [P, GROUPS, P + 2 * W])
        queries = two("queries", [P, BLOCKS, 4, W])
        v_raw = two("v_raw", [WIN, BLOCKS, P])
        v_ones = two("v_ones", [WIN, BLOCKS, GROUPS, VW])
        x_tile = two("x_tile", [P, P])
        row_max = two("row_max", [P, GROUPS * BLOCKS])
        SCORES = GROUPS * BLOCKS * WIN
        arena = sb("arena", [P, 4 * SCORES])
        shifted, probs = ([arena[:, (2 * a + p) * SCORES:(2 * a + p + 1) * SCORES].rearrange("p (k c) -> p k c", c=WIN)
                           for p in range(2)] for a in range(2))
        probsT = [sb(f"probsT{g}", [WIN, BLOCKS, P]) for g in range(GROUPS)]
        rdenom = two("rdenom", [P, 8])
        rdenom_own = two("rdenom_own", [P, 8, 4])
        heads_out = two("heads_out", [P, GROUPS * BLOCKS, W])
        x_all = arena[:, 0:tokens].rearrange("p (n a d) -> p n a d", a=4, d=P)
        x4 = two("x4", [P, 4, P])
        r1_x1 = sb("r1_x1", [P, 4, 4, P])
        r1 = [r1_x1[:, q] for q in range(2)]
        x1 = [r1_x1[:, 2 + q] for q in range(2)]
        x1_b2 = two("x1_b2", [P, 4, P])
        x_lnb = two("x_lnb", [P, 4, P])
        x1T = sb("x1T", [P, 4 * P])
        hidT = sb("hidT", [P, FC, 4 * P])
        r2 = sb("r2", [P, 4, P])
        y2 = sb("y2", [P, 4, P])
        x3 = two("x3", [P, 4, P + 1])
        stats = sb("stats", [P, 12, 6])
        moments = sb("moments", [P, 12, 2])
        var_eps = sb("var_eps", [P, 12])
        rstd = sb("rstd", [P, 12])
        second_moment = sb("second_moment", [P, P + 1])
        prod = sb("prod", [P, PH, P])
        q_mean = sb("q_mean", [P, PH])
        q_mean2 = sb("q_mean2", [P, PH])
        q_var = sb("q_var", [P, PH])
        q_rstd = sb("q_rstd", [P, PH])
        q_scale = sb("q_scale", [P, PH])
        q_shift = sb("q_shift", [P, PH])
        keys_scaled = sb("keys_scaled", [P, PH, KEYS])
        keys_shifted = sb("keys_shifted", [P, PH, KEYS])
        w_sim = sb("w_sim", [P, PH * KEYS])
        c_sim = sb("c_sim", [P, PH * KEYS])
        xT_tile = two("xT_tile", [P, P])
        sim = two("sim", [P, PH, KEYS])
        top = two("top", [P, PH, TOPK])
        top_rel = sb("top_rel", [P, PH, TOPK])
        r3 = prod[:, 0:4, :]
        cand = prod[:, PK_HEADS:PK_HEADS + 4, :].rearrange("p a (b c d) -> p (a b) c d", b=2, c=TOPK)
        best = two("best", [P, PK_HEADS, TOPK])
        best_exp = two("best_exp", [P, PK_HEADS, TOPK])
        z = sb("z", [P, PK_HEADS])
        half_sums = sb("half_sums", [P, PK_HEADS, 4])
        quarter_sums = sb("quarter_sums", [P, PK_HEADS, 2])
        ln_z = sb("ln_z", [P, PK_HEADS])
        last_arg = sb("last_arg", [P, PK_HEADS])
        minus_lnz = two("minus_lnz", [P, PK_HEADS])
        threshold = two("threshold", [P, PK_HEADS])
        sim_rel = sb("sim_rel", [P, PH, KEYS])
        parts = sb("parts", [P, PK_HEADS, 4, KEYS], F16)
        partsT = two("partsT", [P, PK_HEADS, P], F16)
        expgrid = [arena[:, k * EXPERTS:(k + 1) * EXPERTS] for k in range(4)] \
            + [wq_sb[:, k * EXPERTS:(k + 1) * EXPERTS] for k in range(2)] \
            + [wqT_sb[:].rearrange("p a d -> p (a d)")[:, k * EXPERTS:(k + 1) * EXPERTS] for k in range(2)]
        weights = [arena[:, (4 + k) * EXPERTS:(5 + k) * EXPERTS] for k in range(2)] \
            + [r1_x1[:].rearrange("p a b c -> p (a b c)")[:, k * EXPERTS:(k + 1) * EXPERTS] for k in range(2)]
        RING = len(weights)
        act = [hidT[:, 2 * p:2 * p + 2, :].rearrange("p c i -> p (c i)") for p in range(2)]
        gated = prod[:, 0:EC, :]
        out_tile = two("out_tile", [P, P])
        res4 = sb("res4", [P, P])
        stats4 = sb("stats4", [P, 6])
        mom4 = sb("mom4", [P, 2])
        var4 = sb("var4", [P, 1])
        rstd4 = sb("rstd4", [P, 1])

        weights_in = sem("weights_in")
        ident_ready = sem("ident_ready")
        consts_ready = sem("consts_ready")
        band_ready = sem("band_ready")
        band_spread = sem("band_spread")
        mask_ready = sem("mask_ready")
        x4_in = two_sems("x4_in")
        x_all_in = [sem(f"x_all_in{n}") for n in range(NQ)]
        a_transposed = sem("a_transposed")
        a_copied = sem("a_copied")
        v_in = two_sems("v_in")
        x_in = two_sems("x_in")
        operands_ready = sem("operands_ready")
        windows_ready = sem("windows_ready")
        v_ready = sem("v_ready")
        scores_done = sem("scores_done")
        max_done = sem("max_done")
        shift_done = sem("shift_done")
        exp_done = sem("exp_done")
        pt_done = sem("pt_done")
        pt_copied = sem("pt_copied")
        pv_done = sem("pv_done")
        norm_step = sem("norm_step")
        norm_done = sem("norm_done")
        attn_done = sem("attn_done")
        r1_done = sem("r1_done")
        seq = sem("seq")
        r1_staged = sem("r1_staged")
        xlnb_ready = sem("xlnb_ready")
        stat_step = sem("stat_step")
        var_done = sem("var_done")
        rstd_done = sem("rstd_done")
        ln_step = sem("ln_step")
        x1_done = sem("x1_done")
        x1b2_done = sem("x1b2_done")
        x1T_done = sem("x1T_done")
        x1T_copied = sem("x1T_copied")
        ff1_done = sem("ff1_done")
        relu_done = sem("relu_done")
        ff2_done = sem("ff2_done")
        r2_done = sem("r2_done")
        x3_done = sem("x3_done")
        x3_kept = sem("x3_kept")
        x3T_done = sem("x3T_done")
        x3T_copied = sem("x3T_copied")
        gram_done = sem("gram_done")
        r2_normed = sem("r2_normed")
        r2_scaled = sem("r2_scaled")
        r3_done = sem("r3_done")
        moment_ready = sem("moment_ready")
        z_banks = sem("z_banks")
        prod_done = sem("prod_done")
        q_step = sem("q_step")
        q_var_done = sem("q_var_done")
        q_rstd_done = sem("q_rstd_done")
        keys_ready = sem("keys_ready")
        c_row_done = sem("c_row_done")
        w_sim_done = sem("w_sim_done")
        c_sim_copied = sem("c_sim_copied")
        w_sim_copied = sem("w_sim_copied")
        xT_staged = sem("xT_staged")
        down_done = sem("down_done")
        gelu_done = sem("gelu_done")
        sim_done = sem("sim_done")
        sim_copied = sem("sim_copied")
        top_done = sem("top_done")
        top_step = sem("top_step")
        cand_ready = sem("cand_ready")
        best_done = sem("best_done")
        bestexp_done = sem("bestexp_done")
        z_step = sem("z_step")
        z_done = sem("z_done")
        args_done = sem("args_done")
        lnz_done = sem("lnz_done")
        minus_lnz_done = sem("minus_lnz_done")
        threshold_done = sem("threshold_done")
        part_step = sem("part_step")
        parts_done = sem("parts_done")
        partsT_done = sem("partsT_done")
        partsT_copied = sem("partsT_copied")
        grid_done = sem("grid_done")
        gridexp_done = sem("gridexp_done")
        weighed = sem("weighed")
        summed = sem("summed")
        gated_done = sem("gated_done")
        up_done = sem("up_done")
        res_done = sem("res_done")
        d_step = sem("d_step")
        d_var = sem("d_var")
        d_rstd = sem("d_rstd")
        out_ready = sem("out_ready")
        stored = two_sems("stored")

        N_WEIGHTS = 15
        block = ctx.enter_context(nc.Block())

        def need(eng, s, n):
            if not isinstance(n, int) or n > 0:
                eng.wait_ge(s, n)

        def hold(eng):
            eng.sem_inc(seq, 1)

        def over_pairs(eng, n, body):
            body(0, True, False)
            with eng.Fori(1, n - 1) as i:
                body(i, False, False)
            body(n - 1, False, True)

        def bcast(ap, dim, n):
            wide = ap.unsqueeze(dim)
            return wide.broadcast_to([n if d == dim else size for d, size in enumerate(wide.shape)])

        def stretch(ap, n):
            return ap.broadcast_to(list(ap.shape[:-1]) + [n])

        def split(eng, ops, t, p):
            eng.wait_ge(top_done, t + 1)
            hold(eng)
            ops.tensor_tensor(sim_rel[:], sim[p][:], stretch(top[p][:, :, 0:1], KEYS), ALU.subtract
                              ).then_inc(part_step, 1)
            eng.wait_ge(part_step, 3 * t + 1)
            hold(eng)
            ops.tensor_scalar(sim_rel[:], sim_rel[:], FAR, None, ALU.max).then_inc(part_step, 1)
            eng.wait_ge(part_step, 3 * t + 2)
            need(eng, partsT_done, t)
            hold(eng)
            view = parts[:].rearrange("p h (a b) k -> p a b h k", a=2)
            rel = sim_rel[:].rearrange("p (a h) k -> p a h k", a=2)
            ops.tensor_copy(view[:, :, 0], rel).then_inc(part_step, 1)
            eng.wait_ge(part_step, 3 * t + 3)
            hold(eng)
            ops.tensor_tensor(view[:, :, 1], rel, view[:, :, 0], ALU.subtract).then_inc(parts_done, 1)

        def tok(t, n=P):
            return bass.ds(t * P, n)

        @block.sync
        def _(sp):
            for n in range(NQ):
                sp.dma_start(x_all[:, n], x[n * 512:(n + 1) * 512, :].rearrange("(a p) d -> p a d", p=P)
                             ).then_inc(x_all_in[n], 16)

            def load_weights():
                row = lambda v: v.rearrange("(a d) -> a d", a=1).broadcast_to([P, P])
                for dst, src in (
                    (ln1_g_all[:], row(ln1_g)), (ln1_b_all[:], row(ln1_b)), (ln2_g_all[:], row(ln2_g)),
                    (ln2_b_all[:], row(ln2_b)), (b2_all[:], row(b2)),
                    (b1_col[:], b1), (w1_sb[:], w1), (w2_sb[:], w2.rearrange("(c p) d -> p c d", p=P)),
                    (wq_sb[:], w_q), (wqT_sb[:], w_qT), (keysT_sb[:], keysT), (gamma_sb[:], gamma), (beta_sb[:], beta),
                    (downT_sb[:], downT), (up_sb[:], up.rearrange("(c p) d -> p c d", p=P)),
                ):
                    sp.dma_start(dst, src).then_inc(weights_in, 16)

            def b1_loads(i, first, last):
                for p in range(2):
                    t = 2 * i + p
                    need(sp, v_ready, t - 1)
                    for b in range(BLOCKS):
                        sp.dma_start(v_raw[p][:, b, :], x_wrapped[bass.ds(t * P + b * W, WIN), :]).then_inc(v_in[p], 16)
                    need(sp, r1_done, t - 1)
                    sp.dma_start(x_tile[p][:], x[tok(t), :]).then_inc(x_in[p], 16)
                if first:
                    load_weights()

            over_pairs(sp, PAIRS, b1_loads)

            def b2_loads(i, first, last):
                for q in range(2):
                    n = 2 * i + q
                    need(sp, xlnb_ready, n - 1)
                    sp.dma_start(x4[q][:], x[bass.ds(n * 512, 512), :].rearrange("(a p) d -> p a d", p=P)
                                 ).then_inc(x4_in[q], 16)
            over_pairs(sp, NQ // 2, b2_loads)

            def stores(i, first, last):
                for p in range(2):
                    t = 2 * i + p
                    sp.wait_ge(out_ready, t + 1)
                    sp.dma_start(out[tok(t), :], out_tile[p][:]).then_inc(stored[p], 16)
            over_pairs(sp, PAIRS, stores)
            for p in range(2):
                sp.wait_ge(stored[p], 16 * PAIRS + 16)

        @block.gpsimd
        def _(pool):
            nc.gpsimd.memset(minus_half[:], -0.5)
            nc.gpsimd.memset(ones[:], 1.0)
            nc.gpsimd.memset(zeros[:], 0.0)
            nc.gpsimd.memset(xT[:, 0:W], 0.0)
            nc.gpsimd.memset(xT[:, W + tokens:W + tokens + W], 0.0)
            for q in range(2):
                nc.gpsimd.memset(v_ones[q][:], 1.0)
                nc.gpsimd.memset(x3[q][:], 1.0)
            nc.gpsimd.memset(band[:], 0.0)
            nc.gpsimd.memset(ident[:], 0.0).then_inc(ident_ready, 1)
            pool.wait_ge(ident_ready, 1)
            nc.gpsimd.affine_select(out=ident[:], in_=ident[:], compare_op=ALU.not_equal, fill=1.0, base=0,
                                    pattern=[[-1, P]], channel_multiplier=1).then_inc(ident_ready, 1)
            nc.gpsimd.affine_select(out=band[:], in_=band[:], compare_op=ALU.is_ge, fill=MASKED, base=0,
                                    pattern=[[1, WIN]], channel_multiplier=-1).then_inc(band_ready, 1)
            pool.wait_ge(band_ready, 1)
            nc.gpsimd.affine_select(out=band[:], in_=band[:], compare_op=ALU.is_ge, fill=MASKED, base=2 * W,
                                    pattern=[[-1, WIN]], channel_multiplier=1).then_inc(band_ready, 1)
            pool.wait_ge(consts_ready, 6)
            pool.wait_ge(a_copied, NQ)

            def b1_operands(i, first, last):
                for p in range(2):
                    t = 2 * i + p
                    need(pool, scores_done, GROUPS * (t - 1))
                    hold(pool)
                    nc.gpsimd.tensor_copy(own_x[p][:], xT[:, bass.ds(t * P + W, P)]).then_inc(operands_ready, 1)
                    pool.wait_ge(operands_ready, 5 * t + 1)
                    hold(pool)
                    own = own_x[p][:].rearrange("p (b j) -> p b j", b=BLOCKS)
                    for h in range(4):
                        nc.gpsimd.tensor_scalar(queries[p][:, :, h, :], own, head_in_group[:, h:h + 1], None,
                                                ALU.mult).then_inc(operands_ready, 1)
                    need(pool, v_in[p], 16 * BLOCKS * (i + 1))
                    need(pool, pv_done, GROUPS * (t - 1))
                    hold(pool)
                    nc.gpsimd.tensor_copy(v_ones[p][:, :, :, 0:32].rearrange("p b g d -> p (b g) d"),
                                          v_raw[p][:].rearrange("p b (g d) -> p (b g) d", g=GROUPS)).then_inc(v_ready, 1)
            over_pairs(pool, PAIRS, b1_operands)

            pool.wait_ge(weights_in, 16 * N_WEIGHTS)

            def rsqrt(k, lo, hi):
                pool.wait_ge(var_done, k + 1)
                hold(pool)
                nc.gpsimd.tensor_tensor(rstd[:, 4 * lo:4 * hi], var_eps[:, 4 * lo:4 * hi], minus_half[:, 4 * lo:4 * hi],
                                        ALU.pow).then_inc(rstd_done, 1)

            def x_and_bias(n, i, q):
                pool.wait_ge(x4_in[q], 16 * (i + 1))
                need(pool, r3_done, n - 1)
                hold(pool)
                nc.gpsimd.tensor_tensor(x_lnb[q][:], x4[q][:], bcast(ln2_b_all[:], 1, 4), ALU.add
                                        ).then_inc(xlnb_ready, 1)

            def x1_and_bias(n, q):
                pool.wait_ge(x1_done, n + 1)
                need(pool, r2_done, n - 1)
                hold(pool)
                nc.gpsimd.tensor_tensor(x1_b2[q][:], x1[q], bcast(b2_all[:], 1, 4), ALU.add
                                        ).then_inc(x1b2_done, 1)

            rsqrt(0, 1, 3)
            x_and_bias(0, 0, 0)
            x1_and_bias(0, 0)

            def b2_pool(i, first, last):
                for q in range(2):
                    n = 2 * i + q
                    rsqrt(2 * n + 1, 2 if last else 1, 2 if first and q == 0 else 3)
                    rsqrt(2 * n + 2, 0, 1)
                    if not (last and q == 1):
                        x1_and_bias(n + 1, 1 - q)
                        x_and_bias(n + 1, i + q, 1 - q)
            over_pairs(pool, NQ // 2, b2_pool)
            rsqrt(2 * NQ + 1, 2, 3)

            for part, ks in enumerate(Q_SPLIT):
                pool.wait_ge(q_var_done, part + 1)
                hold(pool)
                nc.gpsimd.tensor_tensor(q_rstd[:, ks], q_var[:, ks], minus_half[:, ks], ALU.pow).then_inc(q_rstd_done, 1)

            pool.wait_ge(x3T_copied, NQ)

            def stage_x(t, p):
                need(pool, sim_done, t - 1)
                hold(pool)
                nc.gpsimd.tensor_copy(xT_tile[p][:], xT[:, tok(t)]).then_inc(xT_staged, 1)

            def candidates(t, p):
                pool.wait_ge(top_done, t + 1)
                hold(pool)
                nc.gpsimd.tensor_tensor(top_rel[:], top[p][:], stretch(top[p][:, :, 0:1], TOPK), ALU.subtract
                                        ).then_inc(top_step, 1)
                pool.wait_ge(top_step, t + 1)
                need(pool, best_done, t)
                hold(pool)
                nc.gpsimd.tensor_tensor(cand, bcast(top_rel[:, 0:PK_HEADS, :], 3, TOPK),
                                        bcast(top_rel[:, PK_HEADS:PH, :], 2, TOPK), ALU.add).then_inc(cand_ready, 1)

            def normaliser(t, p):
                pool.wait_ge(bestexp_done, t + 1)
                hold(pool)
                e = best_exp[p]
                nc.gpsimd.tensor_tensor(half_sums[:], e[:, :, 0:4], e[:, :, 4:8], ALU.add).then_inc(z_step, 1)
                pool.wait_ge(z_step, 2 * t + 1)
                hold(pool)
                nc.gpsimd.tensor_tensor(quarter_sums[:], half_sums[:, :, 0:2], half_sums[:, :, 2:4], ALU.add
                                        ).then_inc(z_step, 1)
                pool.wait_ge(z_step, 2 * t + 2)
                hold(pool)
                nc.gpsimd.tensor_tensor(z[:], quarter_sums[:, :, 0], quarter_sums[:, :, 1], ALU.add).then_inc(z_done, 1)
                pool.wait_ge(lnz_done, t + 1)
                need(pool, gridexp_done, PK_HEADS * (t - 1))
                hold(pool)
                nc.gpsimd.tensor_scalar(minus_lnz[p][:], ln_z[:], -1.0, None, ALU.mult).then_inc(minus_lnz_done, 1)
                nc.gpsimd.tensor_scalar(last_arg[:], best[p][:, :, TOPK - 1], 1.0 + SLACK, -SLACK, ALU.mult, ALU.add
                                        ).then_inc(minus_lnz_done, 1)
                pool.wait_ge(minus_lnz_done, 2 * t + 2)
                hold(pool)
                nc.gpsimd.tensor_tensor(last_arg[:], last_arg[:], minus_lnz[p][:], ALU.add).then_inc(args_done, 1)

            stage_x(0, 0)
            stage_x(1, 1)
            candidates(0, 0)
            normaliser(0, 0)

            split(pool, nc.gpsimd, 1, 1)
            candidates(1, 1)

            def d_pool(i, first, last):
                for p in range(2):
                    t = 2 * i + p
                    if not last:
                        stage_x(t + 2, p)
                    if not (first and p == 0):
                        pool.wait_ge(d_var, t)
                        hold(pool)
                        nc.gpsimd.tensor_tensor(rstd4[:], var4[:], minus_half[:, 0:1], ALU.pow).then_inc(d_rstd, 1)
                    if not (last and p == 1):
                        normaliser(t + 1, 1 - p)
                    if not last:
                        split(pool, nc.gpsimd, t + 2, p)
                        candidates(t + 2, p)
            over_pairs(pool, PAIRS, d_pool)
            pool.wait_ge(d_var, NT)
            hold(pool)
            nc.gpsimd.tensor_tensor(rstd4[:], var4[:], minus_half[:, 0:1], ALU.pow).then_inc(d_rstd, 1)

        @block.tensor
        def _(pe):
            pe.wait_ge(ident_ready, 2)

            def a_transpose(n):
                pe.wait_ge(x_all_in[n], 16)
                need(pe, a_copied, n - 1)
                for a in range(4):
                    mm = nc.tensor.transpose(ps[:, n % 2, a * P:(a + 1) * P], x_all[:, n, a, :], ident[:])
                mm.then_inc(a_transposed, 1)

            for n in range(NQ // 2):
                a_transpose(n)
            pe.wait_ge(consts_ready, 6)
            pe.wait_ge(band_ready, 2)
            nc.tensor.matmul(ps[:, 2, 0:WIN], spread4[:], band[:], start=True, stop=True).then_inc(band_spread, 1)
            for n in range(NQ // 2, NQ):
                a_transpose(n)
            pe.wait_ge(mask_ready, 3)

            def scores(t, p, half, mask_at):
                groups = (2 * half, 2 * half + 1)
                if half == 0:
                    pe.wait_ge(operands_ready, 5 * (t + 1))
                    pe.wait_ge(windows_ready, t + 1)
                    if isinstance(t, int) and t == 0:
                        pe.wait_ge(a_copied, NQ)
                need(pe, shift_done, 2 * (t - 1) + half + 1)
                for g in groups:
                    nc.tensor.matmul(ps[:, g, 0:BLOCKS * WIN], ident_bf[:], mask[:, mask_at], start=True, stop=False,
                                     skip_group_check=True)
                for b in range(BLOCKS):
                    for g in groups:
                        mm = nc.tensor.matmul(ps[:, g, b * WIN:(b + 1) * WIN], queries[p][:, b],
                                              windows[p][:, g, b * W:b * W + WIN], start=False, stop=True,
                                              skip_group_check=True)
                        if b == BLOCKS - 1:
                            mm.then_inc(scores_done, 1)

            def probs_transpose(t, p, half):
                pe.wait_ge(exp_done, 2 * t + half + 1)
                if half == 0:
                    need(pe, r1_done, t - 1)
                for g in (2 * half, 2 * half + 1):
                    need(pe, pt_copied, GROUPS * t + g - 1)
                    for b in range(BLOCKS):
                        mm = nc.tensor.transpose(ps[0:WIN, 4 + g % 2, b * P:(b + 1) * P],
                                                 probs[p][:, g * BLOCKS + b, :], ident[:])
                    mm.then_inc(pt_done, 1)

            def values(t, p, half):
                if half == 0:
                    pe.wait_ge(v_ready, t + 1)
                need(pe, norm_done, 2 * (t - 1) + half + 1)
                for g in (2 * half, 2 * half + 1):
                    pe.wait_ge(pt_copied, GROUPS * t + g + 1)
                    for b in range(BLOCKS):
                        k = (g % 2) * BLOCKS + b
                        mm = nc.tensor.matmul(ps[:, 6 + half, k * VW:(k + 1) * VW], probsT[g][:, b, :],
                                              v_ones[p][:, b, g, :], start=True, stop=True)
                    mm.then_inc(pv_done, 1)

            def attn_out(t, p, copied):
                pe.wait_ge(norm_done, 2 * t + 2)
                pe.wait_ge(pt_copied, copied)
                view = heads_out[p][:].rearrange("p (g b) c -> p b g c", g=GROUPS)
                for b in range(BLOCKS):
                    mm = nc.tensor.matmul(ps[32 * b:32 * b + 32, 4, 0:P], fold4[:], view[:, b], start=True, stop=True)
                mm.then_inc(attn_done, 1)

            def mask_of(r):
                return bass.ds(r * BLOCKS * WIN, BLOCKS * WIN)

            def b1_tile(t, p, r_next, first, last):
                more = not (last and p == 1)
                probs_transpose(t, p, 0)
                if more:
                    scores(t + 1, 1 - p, 0, mask_of(r_next))
                probs_transpose(t, p, 1)
                values(t, p, 0)
                if not (first and p == 0):
                    attn_out(t - 1, 1 - p, GROUPS * t + 3)
                if more:
                    scores(t + 1, 1 - p, 1, mask_of(r_next))
                values(t, p, 1)

            for half in range(2):
                scores(0, 0, half, mask_of(0))
            BP = TB // 2
            for p in range(2):
                b1_tile(p, p, p + 1, True, False)
            with pe.Fori(1, BP) as j:
                b1_tile(2 * j, 0, 2 * j + 1, False, False)
                b1_tile(2 * j + 1, 1, (2 * j + 2) % TB, False, False)
            with pe.Fori(1, NT // TB - 1) as s:
                with pe.Fori(0, BP) as j:
                    b1_tile(s * TB + 2 * j, 0, 2 * j + 1, False, False)
                    b1_tile(s * TB + 2 * j + 1, 1, (2 * j + 2) % TB, False, False)
            with pe.Fori(0, BP - 1) as j:
                b1_tile(NT - TB + 2 * j, 0, 2 * j + 1, False, False)
                b1_tile(NT - TB + 2 * j + 1, 1, 2 * j + 2, False, False)
            for p in range(2):
                b1_tile(NT - 2 + p, p, TB - 1, False, True)
            def feed_forward(n, q):
                pe.wait_ge(x1_done, n + 1)
                need(pe, x1T_copied, n)
                for a in range(4):
                    mm = nc.tensor.transpose(ps[:, 0, a * P:(a + 1) * P], x1[q][:, a, :], ident[:])
                mm.then_inc(x1T_done, 1)
                pe.wait_ge(x1T_copied, n + 1)
                for c in range(FC):
                    need(pe, relu_done, FC * n + c - 1)
                    nc.tensor.matmul(ps[:, 1 + c % 2, :], w1_sb[:, c * P:(c + 1) * P], x1T[:], start=True, stop=True
                                     ).then_inc(ff1_done, 1)
                pe.wait_ge(relu_done, FC * (n + 1))
                need(pe, r2_done, n)
                for a in range(4):
                    for c in range(FC):
                        mm = nc.tensor.matmul(ps[:, 3, a * P:(a + 1) * P], hidT[:, c, a * P:(a + 1) * P],
                                              w2_sb[:, c, :], start=(c == 0), stop=(c == FC - 1))
                mm.then_inc(ff2_done, 1)

            pe.wait_ge(weights_in, 16 * N_WEIGHTS)
            pe.wait_ge(shift_done, 2 * NT)
            feed_forward(0, 0)
            attn_out(NT - 1, 1, GROUPS * NT)

            pe.wait_ge(r1_done, NT)
            nc.tensor.matmul(ps[:, 5, 0:P + 1], ident_bf[:], zeros[:], start=True, stop=False,
                             skip_group_check=True)

            def result_products(n, q):
                pe.wait_ge(x3_done, n + 1)
                need(pe, x3T_copied, n)
                for a in range(4):
                    mm = nc.tensor.transpose(ps[:, 4, a * P:(a + 1) * P], x3[q][:, a, 0:P], ident[:])
                mm.then_inc(x3T_done, 1)
                for a in range(4):
                    mm = nc.tensor.matmul(ps[:, 5, 0:P + 1], x3[q][:, a, 0:P], x3[q][:, a, :], start=False, stop=True,
                                          skip_group_check=True)
                mm.then_inc(gram_done, 1)

            def b2_pe(i, first, last):
                for q in range(2):
                    if not (last and q == 1):
                        feed_forward(2 * i + q + 1, 1 - q)
                    if not (first and q == 0):
                        result_products(2 * i + q - 1, 1 - q)
            over_pairs(pe, NQ // 2, b2_pe)
            result_products(NQ - 1, 1)

            pe.wait_ge(moment_ready, 1)
            for k in range(PH):
                if k == 4 * QB:
                    pe.wait_ge(x3T_copied, NQ)
                mm = nc.tensor.matmul(ps[:, k // QB, (k % QB) * (P + 1):(k % QB + 1) * (P + 1)],
                                      wq_sb[:, k * P:(k + 1) * P], second_moment[:], start=True, stop=True)
                if k % QB == QB - 1 or k == PH - 1:
                    mm.then_inc(z_banks, 1)
            for part, ks in enumerate(Q_SPLIT):
                pe.wait_ge(keys_ready, part + 1)
                nc.tensor.matmul(ps[:, 7, ks.start * KEYS:ks.stop * KEYS], ones[:],
                                 keys_shifted[:, ks].rearrange("p a k -> p (a k)"), start=True, stop=True
                                 ).then_inc(c_row_done, 1)
                for k in range(ks.start, ks.stop):
                    mm = nc.tensor.matmul(ps[:, 6, k * KEYS:(k + 1) * KEYS], wqT_sb[:, k, :], keys_scaled[:, k, :],
                                          start=True, stop=True)
            mm.then_inc(w_sim_done, 1)
            pe.wait_ge(c_sim_copied, 1)
            pe.wait_ge(w_sim_copied, 1)

            def down(t, p, sims=0):
                for half in range(2):
                    if p == 1:
                        pe.wait_ge(gelu_done, 2 * t + half - 1)
                    elif half == 0:
                        need(pe, res_done, t)
                    else:
                        pe.wait_ge(partsT_copied, t + 2)
                        pe.wait_ge(sim_copied, sims)
                    for c in range(4 * half, 4 * half + 4):
                        mm = nc.tensor.matmul(ps[:, 6 + half, (c % 4) * P:(c % 4 + 1) * P],
                                              downT_sb[:, c * P:(c + 1) * P], xT[:, tok(t)], start=True, stop=True)
                    mm.then_inc(down_done, 1)

            def similarities(t, p):
                pe.wait_ge(xT_staged, t + 1)
                if isinstance(t, int) and t < 2:
                    need(pe, sim_copied, t)
                else:
                    pe.wait_ge(partsT_copied, t)
                nc.tensor.matmul(ps[:, 7, :], xT_tile[p][:], w_sim[:], start=True, stop=True).then_inc(sim_done, 1)

            def parts_transpose(t, p):
                pe.wait_ge(parts_done, t + 1)
                pe.wait_ge(sim_copied, 2 if isinstance(t, int) and t == 0 else t + 1)
                if p == 0:
                    need(pe, gelu_done, 2 * t)
                bank = ps[:, 7, :].bitcast(F16)
                for h in range(PK_HEADS):
                    mm = nc.tensor.transpose(bank[:, h * P:(h + 1) * P], parts[:, h].rearrange("p a k -> p (a k)"),
                                             ident_h[:])
                mm.then_inc(partsT_done, 1)

            def grid(t, p, h):
                if h == 0:
                    pe.wait_ge(partsT_copied, t + 1)
                need(pe, gridexp_done, PK_HEADS * t + h - 1)
                for half in range(2):
                    mm = nc.tensor.matmul(ps[:, 2 * (h % 2) + half, :], partsT[p][:, h, :],
                                          spread_keys[:, half * 512:(half + 1) * 512], start=True, stop=True)
                mm.then_inc(grid_done, 1)

            def sum_heads(t, h):
                pe.wait_ge(weighed, PK_HEADS * t + h + 1)
                if h == 0:
                    need(pe, gated_done, t)
                for c in range(EC):
                    mm = nc.tensor.matmul(ps[:, 4 + c // 4, (c % 4) * P:(c % 4 + 1) * P],
                                          weights[h % RING][:, c * P:(c + 1) * P], ident[:], is_transpose=True,
                                          start=(h == 0 and c % 4 == 0), stop=(h == PK_HEADS - 1),
                                          skip_group_check=True)
                mm.then_inc(summed, 1)

            def up_projection(t, gelus):
                pe.wait_ge(gated_done, t + 1)
                pe.wait_ge(gelu_done, gelus)
                for c in range(EC):
                    mm = nc.tensor.matmul(ps[:, 6, 0:P], gated[:, c, :], up_sb[:, c, :], start=(c == 0),
                                          stop=(c == EC - 1))
                mm.then_inc(up_done, 1)

            similarities(0, 0)
            similarities(1, 1)
            parts_transpose(0, 0)
            grid(0, 0, 0)
            grid(0, 0, 1)

            def d_pe(i, first, last):
                for p in range(2):
                    t = 2 * i + p
                    more = not (last and p == 1)
                    grid(t, p, 2)
                    grid(t, p, 3)
                    if more:
                        parts_transpose(t + 1, 1 - p)
                    if not (first and p == 0):
                        up_projection(t - 1, 4 * (i + p))
                    grid(t, p, 4)
                    sum_heads(t, 0)
                    grid(t, p, 5)
                    sum_heads(t, 1)
                    grid(t, p, 6)
                    if not last:
                        similarities(t + 2, p)
                    sum_heads(t, 2)
                    grid(t, p, 7)
                    sum_heads(t, 3)
                    if more:
                        grid(t + 1, 1 - p, 0)
                    if p == 0:
                        down(t, 0, NT if last else t + 3)
                    sum_heads(t, 4)
                    if more:
                        grid(t + 1, 1 - p, 1)
                    if p == 0:
                        down(t + 1, 1)
                    sum_heads(t, 5)
                    sum_heads(t, 6)
                    sum_heads(t, 7)
            over_pairs(pe, PAIRS, d_pe)
            up_projection(NT - 1, 2 * NT)

        @block.scalar
        def _(a):
            def copy(out_ap, in_ap):
                return nc.scalar.activation(out_ap, in_ap, ACT.Copy)

            def a_copy(i, first, last):
                for q in range(2):
                    n = 2 * i + q
                    a.wait_ge(a_transposed, n + 1)
                    copy(xT[:, bass.ds(W + n * 512, 512)], ps[:, q, :]).then_inc(a_copied, 1)
            over_pairs(a, NQ // 2, a_copy)

            def exps(t, p):
                for half in range(2):
                    a.wait_ge(shift_done, 2 * t + half + 1)
                    need(a, pt_done, GROUPS * (t - 2) + 2 * half + 2)
                    s = slice(8 * half, 8 * half + 8)
                    nc.scalar.activation(probs[p][:, s, :], shifted[p][:, s, :], ACT.Exp).then_inc(exp_done, 1)

            def probs_copy(t):
                for g in range(GROUPS):
                    a.wait_ge(pt_done, GROUPS * t + g + 1)
                    need(a, pv_done, GROUPS * (t - 1) + g + 1)
                    copy(probsT[g][:].rearrange("p b i -> p (b i)"), ps[0:WIN, 4 + g % 2, :]).then_inc(pt_copied, 1)

            def stage(n, q):
                a.wait_ge(r1_done, 4 * n + 4)
                need(a, x1_done, n - 1)
                copy(r1[q].rearrange("p a d -> p (a d)"), kept[:, bass.ds(n * 512, 512)]).then_inc(r1_staged, 1)

            exps(0, 0)

            def b1_act(i, first, last):
                if last:
                    stage(0, 0)
                    stage(1, 1)
                for p in range(2):
                    probs_copy(2 * i + p)
                    if not (last and p == 1):
                        exps(2 * i + p + 1, 1 - p)
            over_pairs(a, PAIRS, b1_act)

            a.wait_ge(weights_in, 16 * N_WEIGHTS)

            def hidden(n):
                a.wait_ge(x1T_done, n + 1)
                need(a, ff1_done, FC * n)
                copy(x1T[:], ps[:, 0, :]).then_inc(x1T_copied, 1)
                need(a, ff2_done, n)
                for c in range(FC):
                    a.wait_ge(ff1_done, FC * n + c + 1)
                    nc.scalar.activation(hidT[:, c, :], ps[:, 1 + c % 2, :], ACT.Relu, bias=b1_col[:, c:c + 1]
                                         ).then_inc(relu_done, 1)

            def results(n, q):
                a.wait_ge(x3_done, n + 1)
                copy(kept[:, bass.ds(n * 512, 512)].rearrange("p (a d) -> p a d", a=4), x3[q][:, :, 0:P]
                     ).then_inc(x3_kept, 1)
                a.wait_ge(x3T_done, n + 1)
                copy(xT[:, bass.ds(n * 512, 512)], ps[:, 4, :]).then_inc(x3T_copied, 1)

            hidden(0)

            def b2_act(i, first, last):
                for q in range(2):
                    n = 2 * i + q
                    if not last:
                        stage(n + 2, q)
                    if not (last and q == 1):
                        hidden(n + 1)
                    if not (first and q == 0):
                        results(n - 1, 1 - q)
            over_pairs(a, NQ // 2, b2_act)
            results(NQ - 1, 1)

            def gelus(t, p):
                need(a, gated_done, t - 1)
                for half in range(2):
                    a.wait_ge(down_done, 2 * t + half + 1)
                    nc.scalar.activation(act[p][:, half * 512:(half + 1) * 512], ps[:, 6 + half, :],
                                         ACT.Gelu_apprx_tanh).then_inc(gelu_done, 1)

            def best_exps(t, p):
                a.wait_ge(best_done, t + 1)
                nc.scalar.activation(best_exp[p][:], best[p][:], ACT.Exp).then_inc(bestexp_done, 1)

            def log_z(t):
                a.wait_ge(z_done, t + 1)
                nc.scalar.activation(ln_z[:], z[:], ACT.Ln).then_inc(lnz_done, 1)

            def thresholds(t, p):
                a.wait_ge(args_done, t + 1)
                need(a, weighed, PK_HEADS * (t - 1))
                nc.scalar.activation(threshold[p][:], last_arg[:], ACT.Exp).then_inc(threshold_done, 1)

            def parts_copy(t, p):
                a.wait_ge(partsT_done, t + 1)
                copy(partsT[p][:].rearrange("p h i -> p (h i)"), ps[:, 7, :].bitcast(F16)).then_inc(partsT_copied, 1)

            def grid_exp(t, p, h):
                a.wait_ge(grid_done, PK_HEADS * t + h + 1)
                need(a, weighed, PK_HEADS * (t - 1) + h + 1)
                nc.scalar.activation(expgrid[h], ps[:, 2 * (h % 2):2 * (h % 2) + 2, :].rearrange("p a b -> p (a b)"),
                                     ACT.Exp, bias=minus_lnz[p][:, h:h + 1]).then_inc(gridexp_done, 1)

            a.preload_act_table_set(TABLES)
            best_exps(0, 0)
            log_z(0)
            thresholds(0, 0)
            parts_copy(0, 0)

            grid_exp(0, 0, 0)
            grid_exp(0, 0, 1)

            def d_act(i, first, last):
                for p in range(2):
                    t = 2 * i + p
                    more = not (last and p == 1)
                    grid_exp(t, p, 2)
                    grid_exp(t, p, 3)
                    grid_exp(t, p, 4)
                    if more:
                        parts_copy(t + 1, 1 - p)
                    grid_exp(t, p, 5)
                    if more:
                        best_exps(t + 1, 1 - p)
                    grid_exp(t, p, 6)
                    if more:
                        log_z(t + 1)
                    grid_exp(t, p, 7)
                    if more:
                        thresholds(t + 1, 1 - p)
                    if more:
                        grid_exp(t + 1, 1 - p, 0)
                    if p == 0:
                        gelus(t, 0)
                        gelus(t + 1, 1)
                        a.preload_act_table_set(TABLES)
                    if more:
                        grid_exp(t + 1, 1 - p, 1)
            over_pairs(a, PAIRS, d_act)

        @block.vector
        def _(v):
            V = nc.vector
            for p in range(2):
                v.sem_inc(stored[p], 16)
            v.wait_ge(ident_ready, 2)
            V.tensor_reduce(fold4[:], ident[:].rearrange("p (q c) -> p c q", q=4), AX_X, ALU.add).then_inc(consts_ready, 1)
            V.tensor_reduce(quadrant[:], ident[:].rearrange("p (q c) -> p q c", q=4), AX_X, ALU.add
                            ).then_inc(consts_ready, 1)
            V.tensor_reduce(head16[:], ident[:].rearrange("p (h e) -> p h e", e=DH), AX_X, ALU.add
                            ).then_inc(consts_ready, 1)
            V.tensor_copy(spread4[:].rearrange("p (q c) -> p q c", q=4), bcast(ident[0:W, 0:W], 1, 4)
                          ).then_inc(consts_ready, 1)
            V.tensor_copy(ident_bf[:], ident[:]).then_inc(consts_ready, 1)
            v.wait_ge(consts_ready, 5)
            V.tensor_reduce(head_in_group[:], head16[:].rearrange("p (q h) -> p h q", q=4), AX_X, ALU.add
                            ).then_inc(consts_ready, 1)
            V.tensor_copy(ident_h[:], ident[:])
            for q in range(4):
                rows = slice(32 * q, 32 * q + 32)
                one = ident[rows, 32 * q:32 * q + 32]
                V.tensor_copy(spread_keys[rows, :].rearrange("p (i j) -> p i j", i=KEYS),
                              bcast(one, 2, KEYS) if q < 2 else bcast(one, 1, KEYS))
            v.wait_ge(band_spread, 1)
            m = mask[:].rearrange("p (b c) -> p b c", c=WIN)
            V.tensor_copy(m, bcast(ps[:, 2, 0:WIN], 1, TB * BLOCKS)).then_inc(mask_ready, 1)
            v.wait_ge(mask_ready, 1)
            V.memset(m[:, 0, 0:W], MASKED).then_inc(mask_ready, 1)
            V.memset(m[:, TB * BLOCKS - 1, 2 * W:WIN], MASKED).then_inc(mask_ready, 1)

            def shift(t, p, half):
                at = 8 * half
                sc = ps[:, 2 * half:2 * half + 2, 0:BLOCKS * WIN].rearrange("p a (b c) -> p a b c", c=WIN)
                mx = row_max[p][:, at:at + 8]
                v.wait_ge(scores_done, GROUPS * t + 2 * half + 2)
                V.tensor_reduce(mx.rearrange("p (a b) -> p a b", a=2), sc, AX_X, ALU.max).then_inc(max_done, 1)
                v.wait_ge(max_done, 2 * t + half + 1)
                need(v, exp_done, 2 * (t - 2) + half + 1)
                V.tensor_tensor(shifted[p][:, at:at + 8, :].rearrange("p (a b) c -> p a b c", a=2), sc,
                                bcast(mx.rearrange("p (a b) -> p a b", a=2), 3, WIN), ALU.subtract
                                ).then_inc(shift_done, 1)

            def normalise(t, p, half):
                pv = ps[:, 6 + half, 0:8 * VW].rearrange("p (k c) -> p k c", c=VW)
                n = 2 * t + half
                v.wait_ge(pv_done, GROUPS * t + 2 * half + 2)
                V.reciprocal(rdenom[half][:], pv[:, :, 32]).then_inc(norm_step, 1)
                v.wait_ge(norm_step, 2 * n + 1)
                V.tensor_tensor(rdenom_own[half][:], bcast(rdenom[half][:], 2, 4), bcast(quadrant[:], 1, 8), ALU.mult
                                ).then_inc(norm_step, 1)
                v.wait_ge(norm_step, 2 * n + 2)
                if half == 0:
                    need(v, attn_done, t - 1)
                V.tensor_tensor(heads_out[p][:, 8 * half:8 * half + 8, :].rearrange("p k (h d) -> p k h d", h=4),
                                pv[:, :, 0:32].rearrange("p k (h d) -> p k h d", h=4),
                                bcast(rdenom_own[half][:], 3, DH), ALU.mult).then_inc(norm_done, 1)

            def residual(t, i, p):
                v.wait_ge(attn_done, t + 1)
                v.wait_ge(x_in[p], 16 * (i + 1))
                V.tensor_tensor(kept[:, tok(t)], ps[:, 4, 0:P], x_tile[p][:], ALU.add).then_inc(r1_done, 1)

            def group_windows(t, p):
                need(v, scores_done, GROUPS * (t - 1))
                V.tensor_tensor(windows[p][:], bcast(xT[:, tok(t, P + 2 * W)], 1, GROUPS),
                                bcast(quadrant[:], 2, P + 2 * W), ALU.mult).then_inc(windows_ready, 1)

            v.wait_ge(a_copied, NQ)
            group_windows(0, 0)
            group_windows(1, 1)
            shift(0, 0, 0)
            shift(0, 0, 1)

            def ln_stats(norm, src):
                for a in range(4):
                    last = V.bn_stats(stats[:, 4 * norm + a, :], src[:, a, :])
                return last

            def ln_moments(k, lo, hi):
                v.wait_ge(stat_step, 2 * k + 1)
                hold(v)
                for j in range(4 * lo, 4 * hi):
                    last = V.bn_aggr(moments[:, j, :], stats[:, j, :])
                last.then_inc(stat_step, 1)
                v.wait_ge(stat_step, 2 * k + 2)
                V.tensor_scalar(var_eps[:, 4 * lo:4 * hi], moments[:, 4 * lo:4 * hi, 1], EPS, None, ALU.add
                                ).then_inc(var_done, 1)

            def ln_apply(norm, src, dst, done):
                for a in range(4):
                    j = 4 * norm + a
                    last = V.tensor_scalar(dst[:, a, :], src[:, a, :], moments[:, j, 0:1], rstd[:, j:j + 1],
                                           ALU.subtract, ALU.mult)
                last.then_inc(done, 1)

            def ln1_stats(n, q, place=1):
                v.wait_ge(r1_staged, n + 1)
                return ln_stats(place, r1[q])

            def ln1_apply(n, q, place=1):
                ln_apply(place, r1[q], y2, ln_step)
                v.wait_ge(ln_step, 2 * n + 1)
                V.tensor_tensor(y2[:], y2[:], bcast(ln1_g_all[:], 1, 4), ALU.mult).then_inc(ln_step, 1)
                v.wait_ge(ln_step, 2 * n + 2)
                need(v, x1b2_done, n - 1)
                need(v, x1T_done, n - 1)
                V.tensor_tensor(x1[q], y2[:], bcast(ln1_b_all[:], 1, 4), ALU.add).then_inc(x1_done, 1)

            def ln2_stats(n, q):
                v.wait_ge(ff2_done, n + 1)
                v.wait_ge(x1b2_done, n + 1)
                V.tensor_tensor(r2[:], ps[:, 3, :].rearrange("p (a d) -> p a d", a=4), x1_b2[q][:], ALU.add
                                ).then_inc(r2_done, 1)
                v.wait_ge(r2_done, n + 1)
                return ln_stats(0, r2)

            def ln2_apply(n, q):
                ln_apply(0, r2, r2, r2_normed)
                v.wait_ge(r2_normed, n + 1)
                V.tensor_tensor(r2[:], r2[:], bcast(ln2_g_all[:], 1, 4), ALU.mult).then_inc(r2_scaled, 1)
                v.wait_ge(r2_scaled, n + 1)
                v.wait_ge(xlnb_ready, n + 1)
                V.tensor_tensor(r3, r2[:], x_lnb[q][:], ALU.add).then_inc(r3_done, 1)

            def ln3_stats(n):
                v.wait_ge(r3_done, n + 1)
                return ln_stats(2, r3)

            def ln3_apply(n, q):
                need(v, gram_done, n - 1)
                need(v, x3_kept, n - 1)
                ln_apply(2, r3, x3[q][:, :, 0:P], x3_done)

            def b1_dve(i, first, last):
                if last:
                    v.wait_ge(weights_in, 16 * N_WEIGHTS)
                    ln1_stats(0, 0)
                    ln1_stats(1, 1, 2).then_inc(stat_step, 1)
                    ln_moments(0, 1, 3)
                for p in range(2):
                    t = 2 * i + p
                    if not (last and p == 1):
                        shift(t + 1, 1 - p, 0)
                    if not last:
                        group_windows(t + 2, p)
                    normalise(t, p, 0)
                    if not (first and p == 0):
                        residual(t - 1, i if p == 1 else i - 1, 1 - p)
                    if not (last and p == 1):
                        shift(t + 1, 1 - p, 1)
                    normalise(t, p, 1)
                    if last and p == 0:
                        v.wait_ge(rstd_done, 1)
                        ln1_apply(0, 0)
            over_pairs(v, PAIRS, b1_dve)
            residual(NT - 1, PAIRS - 1, 1)

            ln1_apply(1, 1, 2)

            def b2_dve(i, first, last):
                for q in range(2):
                    n = 2 * i + q
                    with_ln3 = not (first and q == 0)
                    if with_ln3:
                        step = ln3_stats(n - 1)
                    if not last:
                        step = ln1_stats(n + 2, q)
                    step.then_inc(stat_step, 1)
                    ln_moments(2 * n + 1, 2 if last else 1, 3 if with_ln3 else 2)
                    ln2_stats(n, q).then_inc(stat_step, 1)
                    ln_moments(2 * n + 2, 0, 1)
                    v.wait_ge(rstd_done, 2 * n + 2)
                    if not last:
                        ln1_apply(n + 2, q)
                    if with_ln3:
                        ln3_apply(n - 1, 1 - q)
                    v.wait_ge(rstd_done, 2 * n + 3)
                    ln2_apply(n, q)
            over_pairs(v, NQ // 2, b2_dve)
            ln3_stats(NQ - 1).then_inc(stat_step, 1)
            ln_moments(2 * NQ + 1, 2, 3)
            v.wait_ge(rstd_done, 2 * NQ + 2)
            ln3_apply(NQ - 1, 1)

            v.wait_ge(gram_done, NQ)
            V.tensor_scalar(second_moment[:], ps[:, 5, 0:P + 1], 1.0 / tokens, None, ALU.mult).then_inc(moment_ready, 1)

            def q_moments(b):
                n = min(QB, PH - QB * b)
                v.wait_ge(z_banks, b + 1)
                z3 = ps[:, b, 0:n * (P + 1)].rearrange("p (k c) -> p k c", c=P + 1)
                V.tensor_copy(q_mean[:, QB * b:QB * b + n], z3[:, :, P])
                V.tensor_tensor(prod[:, QB * b:QB * b + n, :], z3[:, :, 0:P], wqT_sb[:, QB * b:QB * b + n, :], ALU.mult
                                ).then_inc(prod_done, 1)

            def q_sums(b):
                n = min(QB, PH - QB * b)
                v.wait_ge(prod_done, b + 1)
                return V.tensor_reduce(q_var[:, QB * b:QB * b + n], prod[:, QB * b:QB * b + n, :], AX_X, ALU.add)

            def q_variance(part):
                ks = Q_SPLIT[part]
                V.tensor_tensor(q_mean2[:, ks], q_mean[:, ks], q_mean[:, ks], ALU.mult).then_inc(q_step, 1)
                v.wait_ge(q_step, 3 * part + 2)
                V.tensor_tensor(q_var[:, ks], q_var[:, ks], q_mean2[:, ks], ALU.subtract).then_inc(q_step, 1)
                v.wait_ge(q_step, 3 * part + 3)
                V.tensor_scalar(q_var[:, ks], q_var[:, ks], 0.0, EPS, ALU.max, ALU.add).then_inc(q_var_done, 1)

            def scale_keys(part):
                ks = Q_SPLIT[part]
                v.wait_ge(q_rstd_done, part + 1)
                V.tensor_tensor(q_scale[:, ks], q_rstd[:, ks], gamma_sb[:, ks], ALU.mult).then_inc(q_step, 1)
                v.wait_ge(q_step, 6 + 3 * part + 1)
                V.tensor_tensor(q_shift[:, ks], q_mean[:, ks], q_scale[:, ks], ALU.mult).then_inc(q_step, 1)
                v.wait_ge(q_step, 6 + 3 * part + 2)
                V.tensor_tensor(q_shift[:, ks], beta_sb[:, ks], q_shift[:, ks], ALU.subtract).then_inc(q_step, 1)
                V.tensor_tensor(keys_scaled[:, ks], keysT_sb[:, ks], bcast(q_scale[:, ks], 2, KEYS), ALU.mult)
                v.wait_ge(q_step, 6 + 3 * part + 3)
                V.tensor_tensor(keys_shifted[:, ks], keysT_sb[:, ks], bcast(q_shift[:, ks], 2, KEYS), ALU.mult
                                ).then_inc(keys_ready, 1)

            for b in range(6):
                q_moments(b)
                if b % 3:
                    q_sums(b - 1)
                if b % 3 == 2:
                    q_sums(b).then_inc(q_step, 1)
                    q_variance(b // 3)
            for part in range(2):
                scale_keys(part)
            v.wait_ge(c_row_done, 2)
            V.tensor_copy(c_sim[:], ps[:, 7, :]).then_inc(c_sim_copied, 1)
            v.wait_ge(w_sim_done, 1)
            V.tensor_copy(w_sim[:], ps[:, 6, :]).then_inc(w_sim_copied, 1)
            v.wait_ge(c_sim_copied, 1)

            def top_keys(t, p):
                v.wait_ge(sim_done, t + 1)
                need(v, part_step, 3 * (t - 2) + 1)
                V.tensor_tensor(sim[p][:].rearrange("p a k -> p (a k)"), ps[:, 7, :], c_sim[:], ALU.add
                                ).then_inc(sim_copied, 1)
                v.wait_ge(sim_copied, t + 1)
                hold(v)
                for k in range(PH):
                    last = V.max(top[p][:, k, :], sim[p][:, k, :])
                last.then_inc(top_done, 1)

            def top_pairs(t, p):
                v.wait_ge(cand_ready, t + 1)
                hold(v)
                for h in range(PK_HEADS):
                    last = V.max(best[p][:, h, :], cand[:, h].rearrange("p a b -> p (a b)"))
                last.then_inc(best_done, 1)

            def weigh(t, p, h):
                v.wait_ge(gridexp_done, PK_HEADS * t + h + 1)
                need(v, summed, PK_HEADS * t + h + 1 - RING)
                if h == 0:
                    v.wait_ge(threshold_done, t + 1)
                V.scalar_tensor_tensor(weights[h % RING], expgrid[h], threshold[p][:, h:h + 1], expgrid[h],
                                       ALU.is_ge, ALU.mult).then_inc(weighed, 1)

            def gate(t, p):
                v.wait_ge(summed, PK_HEADS * (t + 1))
                v.wait_ge(gelu_done, 2 * t + 2)
                need(v, up_done, t)
                V.tensor_tensor(gated.rearrange("p c i -> p (c i)"), ps[:, 4:6, :].rearrange("p a b -> p (a b)"),
                                act[p], ALU.mult).then_inc(gated_done, 1)

            def last_moments(t):
                v.wait_ge(up_done, t + 1)
                V.tensor_tensor(res4[:], ps[:, 6, 0:P], kept[:, tok(t)], ALU.add).then_inc(res_done, 1)
                v.wait_ge(res_done, t + 1)
                V.bn_stats(stats4[:], res4[:]).then_inc(d_step, 1)
                v.wait_ge(d_step, 2 * t + 1)
                hold(v)
                V.bn_aggr(mom4[:], stats4[:]).then_inc(d_step, 1)
                v.wait_ge(d_step, 2 * t + 2)
                V.tensor_scalar(var4[:], mom4[:, 1:2], EPS, None, ALU.add).then_inc(d_var, 1)

            def last_norm(t, i, p):
                v.wait_ge(d_rstd, t + 1)
                v.wait_ge(stored[p], 16 * i + 16)
                V.tensor_scalar(out_tile[p][:], res4[:], mom4[:, 0:1], rstd4[:], ALU.subtract, ALU.mult
                                ).then_inc(out_ready, 1)

            v.wait_ge(x3_kept, NQ)
            top_keys(0, 0)
            split(v, V, 0, 0)
            top_pairs(0, 0)
            top_keys(1, 1)
            weigh(0, 0, 0)

            def d_dve(i, first, last):
                for p in range(2):
                    t = 2 * i + p
                    more = not (last and p == 1)
                    before = not (first and p == 0)
                    weigh(t, p, 1)
                    weigh(t, p, 2)
                    if before:
                        last_moments(t - 1)
                    if more:
                        top_pairs(t + 1, 1 - p)
                    weigh(t, p, 3)
                    weigh(t, p, 4)
                    if not last:
                        top_keys(t + 2, p)
                    weigh(t, p, 5)
                    weigh(t, p, 6)
                    weigh(t, p, 7)
                    if before:
                        last_norm(t - 1, i if p == 1 else i - 1, 1 - p)
                    if more:
                        weigh(t + 1, 1 - p, 0)
                    gate(t, p)
            over_pairs(v, PAIRS, d_dve)
            last_moments(NT - 1)
            last_norm(NT - 1, PAIRS - 1, 1)


_OUT = ((4, 1024, 128), "float32")


def kernel(**inputs):
    import numpy as np
    import concourse.bacc as bacc
    from concourse.bass_utils import run_bass_kernel_spmd

    a = {k: np.asarray(v) for k, v in inputs.items()}
    x = a["L0_attn_src"].reshape(4096, 128)
    arrays = {
        "x": x,
        "x_wrapped": np.concatenate([x[-W:], x, x[:W]]),
        "ln1_g": a["L0_attn_ln1_g"], "ln1_b": a["L0_attn_ln1_b"],
        "ln2_g": a["L0_attn_ln2_g"], "ln2_b": a["L0_attn_ln2_b"],
        "w1": a["L0_attn_W1"], "b1": a["L0_attn_b1"].reshape(FC, P).T,
        "w2": a["L0_attn_W2"], "b2": a["L0_attn_b2"],
        "w_q": a["L0_ffn_w_q"], "w_qT": a["L0_ffn_w_q"].reshape(P, PH, P).transpose(2, 1, 0),
        "gamma": a["L0_ffn_bn_gamma"].reshape(PH, P).T, "beta": a["L0_ffn_bn_beta"].reshape(PH, P).T,
        "keysT": a["L0_ffn_keys"].transpose(3, 2, 0, 1).reshape(P, PH, KEYS),
        "downT": a["L0_ffn_down_embed"].T, "up": a["L0_ffn_up_embed"],
    }
    arrays = {f"in_{k}": np.ascontiguousarray(v) for k, v in arrays.items()}
    nc = bacc.Bacc("TRN2", target_bir_lowering=False, num_devices=1)
    args = [nc.dram_tensor(k, v.shape, mybir.dt.from_np(v.dtype), kind="ExternalInput").ap() for k, v in arrays.items()]
    out = nc.dram_tensor("out", (4096, 128), F32, kind="ExternalOutput").ap()
    attention_and_product_keys(nc, *args, out)
    r = run_bass_kernel_spmd(nc, [arrays], core_ids=[0])
    return r.results[0]["out"].reshape(_OUT[0])
```
